# Optimizing a Trainium2 kernel written in Bass

```python
import numpy as np
import jax
import jax.numpy as jnp

def _softmax(x, axis=-1):
    return jax.nn.softmax(x, axis=axis)

def _gelu(x):
    return jax.nn.gelu(x, approximate=True)

def _silu(x):
    return jax.nn.silu(x)

def _sigmoid(x):
    return jax.nn.sigmoid(x)

def _layernorm(x, axis=-1, eps=1e-05):
    m = jnp.mean(x, axis=axis, keepdims=True)
    v = jnp.var(x, axis=axis, keepdims=True)
    return (x - m) / jnp.sqrt(v + eps)

def _scatter_add(tgt, idx, src, axis=0):
    return tgt.at[idx].add(src)

def _segment_sum(src, seg, n):
    return jax.ops.segment_sum(src, seg, n)
kernel_name = 'mk_hybrid_d1_jaxref_r8_da6df3'

def setup_inputs(seed: int=0):
    np.random.seed(seed)
    _w = jnp.asarray

    def _L0_attn_a_setup():
        import jax, jax.numpy as jnp
        import numpy as np
        B, T, C, H = (8, 256, 128, 16)
        S = C // H
        LN_EPS = 1e-05
        key = jax.random.key(seed)
        ks = jax.random.split(key, 12)
        w = lambda k: jax.random.normal(k, (C, C), dtype=jnp.float32) * 0.02
        return {'x': jax.random.normal(ks[0], (B, T, C), dtype=jnp.float32), 'time_mix_k': jax.random.uniform(ks[1], (1, 1, C), dtype=jnp.float32), 'time_mix_v': jax.random.uniform(ks[2], (1, 1, C), dtype=jnp.float32), 'time_mix_r': jax.random.uniform(ks[3], (1, 1, C), dtype=jnp.float32), 'time_decay': -jax.random.uniform(ks[4], (H, S), minval=0.1, maxval=5.0, dtype=jnp.float32), 'time_first': jax.random.uniform(ks[5], (H, S), dtype=jnp.float32), 'Wk': w(ks[6]), 'Wv': w(ks[7]), 'Wr': w(ks[8]), 'Wo': w(ks[9]), 'ln_g': jnp.ones((C,), jnp.float32), 'ln_b': jnp.zeros((C,), jnp.float32)}
    _L0_attn_a_in = _L0_attn_a_setup()

    def _L0_attn_b_setup():
        import jax, jax.numpy as jnp
        import numpy as np
        H_HEADS = 16
        DECAY_C = 0.7408182206817179

        def _gelu(x):
            return jax.nn.gelu(x, approximate=False)

        def _mlp(x, W1, b1, W2, b2):
            return _gelu(x @ W1 + b1) @ W2 + b2

        def _forward(queries, mu_r, mu_k, mu_v, mu_g, mu_a, mu_d, dA, dB, db, aA, aB, ab, gA, gB, rW1, rb1, rW2, rb2, kW1, kb1, kW2, kb2, vW1, vb1, vW2, vb2, oW1, ob1, oW2, ob2, rem_mult, iclr_mix, bonus_mult, ln_g, ln_b):
            B, T, C = queries.shape
            H = H_HEADS
            N = C // H
            r = _mlp(queries + mu_r, rW1, rb1, rW2, rb2)
            k = _mlp(queries + mu_k, kW1, kb1, kW2, kb2)
            v = _mlp(queries + mu_v, vW1, vb1, vW2, vb2)
            gate = jax.nn.sigmoid((queries + mu_g) @ gA @ gB)
            iclr = jax.nn.sigmoid((queries + mu_a) @ aA @ ab + (queries + mu_a) @ aA @ aB) if False else jax.nn.sigmoid((queries + mu_a) @ aA @ aB + ab)
            decay = jnp.exp(-DECAY_C * jax.nn.sigmoid(jnp.tanh((queries + mu_d) @ dA @ dB + db)))
            removal_k = k * rem_mult
            replacement_k = k * (1.0 + (iclr - 1.0) * iclr_mix)
            rh = r.reshape(B, T, H, N)
            rkh = replacement_k.reshape(B, T, H, N)
            vh = v.reshape(B, T, H, N)
            dh = decay.reshape(B, T, H, N)
            ah = iclr.reshape(B, T, H, N)
            rmh = removal_k.reshape(B, T, H, N)
            kn = rmh / jnp.maximum(jnp.linalg.norm(rmh, axis=-1, keepdims=True), 1e-12)
            xs = tuple((jnp.swapaxes(a, 0, 1) for a in (dh, ah, kn, rkh, vh, rh)))

            def step(wkv, x):
                d, a, knt, rk, vt, rt = x
                tmp = jnp.einsum('bhj,bhjk->bhk', a * knt, wkv)
                wkv = d[..., None] * wkv - knt[..., None] * tmp[:, :, None, :] + vt[..., None] * rk[:, :, None, :]
                return (wkv, jnp.einsum('bhij,bhj->bhi', wkv, rt))
            wkv0 = jnp.zeros((B, H, N, N), queries.dtype)
            _, out_t = jax.lax.scan(step, wkv0, xs)
            out = jnp.swapaxes(out_t, 0, 1)
            bonus = jnp.sum(rh * rkh, -1, keepdims=True) * 0.2 * vh * bonus_mult.reshape(1, 1, H, N)
            out = (out + bonus).reshape(B, T, C)
            mu = jnp.mean(out, -1, keepdims=True)
            var = jnp.mean((out - mu) ** 2, -1, keepdims=True)
            out = (out - mu) / jnp.sqrt(var + 1e-06) * ln_g + ln_b
            out = out * gate
            out = _mlp(out, oW1, ob1, oW2, ob2)
            return out
        B, T, C = (4, 256, 128)
        L = max(64, C // 8)
        E = int(C * 1.2)
        key = jax.random.key(seed)
        ctr = [0]

        def rn(shape, s=0.02):
            ctr[0] += 1
            return jax.random.normal(jax.random.fold_in(key, ctr[0]), shape, jnp.float32) * s
        z = lambda *s: jnp.zeros(s, jnp.float32)
        inp = {'queries': rn((B, T, C), 1.0), 'keys': rn((B, T, C), 1.0), 'values': rn((B, T, C), 1.0), 'attn_mask': jnp.ones((B, T), dtype=bool), 'mu_r': rn((C,)), 'mu_k': rn((C,)), 'mu_v': rn((C,)), 'mu_g': rn((C,)), 'mu_a': rn((C,)), 'mu_d': rn((C,)), 'dA': rn((C, L)), 'dB': rn((L, C)), 'db': z(C), 'aA': rn((C, L)), 'aB': rn((L, C)), 'ab': z(C), 'gA': rn((C, L)), 'gB': rn((L, C)), 'rW1': rn((C, E)), 'rb1': z(E), 'rW2': rn((E, C)), 'rb2': z(C), 'kW1': rn((C, E)), 'kb1': z(E), 'kW2': rn((E, C)), 'kb2': z(C), 'vW1': rn((C, E)), 'vb1': z(E), 'vW2': rn((E, C)), 'vb2': z(C), 'oW1': rn((C, E)), 'ob1': z(E), 'oW2': rn((E, C)), 'ob2': z(C), 'rem_mult': rn((C,), 0.05), 'iclr_mix': jnp.full((C,), 0.7, jnp.float32), 'bonus_mult': jnp.full((C,), 1.2, jnp.float32), 'ln_g': jnp.ones((C,), jnp.float32), 'ln_b': z(C)}
        return inp
    _L0_attn_b_in = _L0_attn_b_setup()

    def _L0_ffn_setup():
        import jax, jax.numpy as jnp
        import numpy as np
        B, S, H = (2, 128, 128)
        E, F = (8, 512)
        GATE_TEMP = 0.1
        key = jax.random.key(seed)
        ks = jax.random.split(key, 6)
        s_h = 1.0 / np.sqrt(H)
        s_f = 1.0 / np.sqrt(F)
        return {'hidden_states': jax.random.normal(ks[0], (B, S, H), dtype=jnp.float32), 'w_router': jax.random.normal(ks[1], (H, E), dtype=jnp.float32) * s_h, 'w_gating': jax.random.normal(ks[2], (H, E), dtype=jnp.float32) * s_h, 'w_gate': jax.random.normal(ks[3], (E, H, F), dtype=jnp.float32) * s_h, 'w_up': jax.random.normal(ks[4], (E, H, F), dtype=jnp.float32) * s_h, 'w_down': jax.random.normal(ks[5], (E, F, H), dtype=jnp.float32) * s_f}
    _L0_ffn_in = _L0_ffn_setup()
    _d = {'L0_attn_a_x': _L0_attn_a_in['x'], 'L0_attn_a_time_mix_k': _L0_attn_a_in['time_mix_k'], 'L0_attn_a_time_mix_v': _L0_attn_a_in['time_mix_v'], 'L0_attn_a_time_mix_r': _L0_attn_a_in['time_mix_r'], 'L0_attn_a_time_decay': _L0_attn_a_in['time_decay'], 'L0_attn_a_time_first': _L0_attn_a_in['time_first'], 'L0_attn_a_Wk': _L0_attn_a_in['Wk'], 'L0_attn_a_Wv': _L0_attn_a_in['Wv'], 'L0_attn_a_Wr': _L0_attn_a_in['Wr'], 'L0_attn_a_Wo': _L0_attn_a_in['Wo'], 'L0_attn_a_ln_g': _L0_attn_a_in['ln_g'], 'L0_attn_a_ln_b': _L0_attn_a_in['ln_b'], 'L0_attn_b_keys': _L0_attn_b_in['keys'], 'L0_attn_b_values': _L0_attn_b_in['values'], 'L0_attn_b_attn_mask': _L0_attn_b_in['attn_mask'], 'L0_attn_b_mu_r': _L0_attn_b_in['mu_r'], 'L0_attn_b_mu_k': _L0_attn_b_in['mu_k'], 'L0_attn_b_mu_v': _L0_attn_b_in['mu_v'], 'L0_attn_b_mu_g': _L0_attn_b_in['mu_g'], 'L0_attn_b_mu_a': _L0_attn_b_in['mu_a'], 'L0_attn_b_mu_d': _L0_attn_b_in['mu_d'], 'L0_attn_b_dA': _L0_attn_b_in['dA'], 'L0_attn_b_dB': _L0_attn_b_in['dB'], 'L0_attn_b_db': _L0_attn_b_in['db'], 'L0_attn_b_aA': _L0_attn_b_in['aA'], 'L0_attn_b_aB': _L0_attn_b_in['aB'], 'L0_attn_b_ab': _L0_attn_b_in['ab'], 'L0_attn_b_gA': _L0_attn_b_in['gA'], 'L0_attn_b_gB': _L0_attn_b_in['gB'], 'L0_attn_b_rW1': _L0_attn_b_in['rW1'], 'L0_attn_b_rb1': _L0_attn_b_in['rb1'], 'L0_attn_b_rW2': _L0_attn_b_in['rW2'], 'L0_attn_b_rb2': _L0_attn_b_in['rb2'], 'L0_attn_b_kW1': _L0_attn_b_in['kW1'], 'L0_attn_b_kb1': _L0_attn_b_in['kb1'], 'L0_attn_b_kW2': _L0_attn_b_in['kW2'], 'L0_attn_b_kb2': _L0_attn_b_in['kb2'], 'L0_attn_b_vW1': _L0_attn_b_in['vW1'], 'L0_attn_b_vb1': _L0_attn_b_in['vb1'], 'L0_attn_b_vW2': _L0_attn_b_in['vW2'], 'L0_attn_b_vb2': _L0_attn_b_in['vb2'], 'L0_attn_b_oW1': _L0_attn_b_in['oW1'], 'L0_attn_b_ob1': _L0_attn_b_in['ob1'], 'L0_attn_b_oW2': _L0_attn_b_in['oW2'], 'L0_attn_b_ob2': _L0_attn_b_in['ob2'], 'L0_attn_b_rem_mult': _L0_attn_b_in['rem_mult'], 'L0_attn_b_iclr_mix': _L0_attn_b_in['iclr_mix'], 'L0_attn_b_bonus_mult': _L0_attn_b_in['bonus_mult'], 'L0_attn_b_ln_g': _L0_attn_b_in['ln_g'], 'L0_attn_b_ln_b': _L0_attn_b_in['ln_b'], 'L0_ffn_w_router': _L0_ffn_in['w_router'], 'L0_ffn_w_gating': _L0_ffn_in['w_gating'], 'L0_ffn_w_gate': _L0_ffn_in['w_gate'], 'L0_ffn_w_up': _L0_ffn_in['w_up'], 'L0_ffn_w_down': _L0_ffn_in['w_down']}
    _x0 = _d['L0_attn_a_x']
    _d['L0_attn_a_x'] = jax.random.normal(jax.random.fold_in(jax.random.key(seed), 1), (2, 1024, 128), dtype=_x0.dtype)
    del _x0
    return _d

def reference(L0_attn_a_x, L0_attn_a_time_mix_k, L0_attn_a_time_mix_v, L0_attn_a_time_mix_r, L0_attn_a_time_decay, L0_attn_a_time_first, L0_attn_a_Wk, L0_attn_a_Wv, L0_attn_a_Wr, L0_attn_a_Wo, L0_attn_a_ln_g, L0_attn_a_ln_b, L0_attn_b_keys, L0_attn_b_values, L0_attn_b_attn_mask, L0_attn_b_mu_r, L0_attn_b_mu_k, L0_attn_b_mu_v, L0_attn_b_mu_g, L0_attn_b_mu_a, L0_attn_b_mu_d, L0_attn_b_dA, L0_attn_b_dB, L0_attn_b_db, L0_attn_b_aA, L0_attn_b_aB, L0_attn_b_ab, L0_attn_b_gA, L0_attn_b_gB, L0_attn_b_rW1, L0_attn_b_rb1, L0_attn_b_rW2, L0_attn_b_rb2, L0_attn_b_kW1, L0_attn_b_kb1, L0_attn_b_kW2, L0_attn_b_kb2, L0_attn_b_vW1, L0_attn_b_vb1, L0_attn_b_vW2, L0_attn_b_vb2, L0_attn_b_oW1, L0_attn_b_ob1, L0_attn_b_oW2, L0_attn_b_ob2, L0_attn_b_rem_mult, L0_attn_b_iclr_mix, L0_attn_b_bonus_mult, L0_attn_b_ln_g, L0_attn_b_ln_b, L0_ffn_w_router, L0_ffn_w_gating, L0_ffn_w_gate, L0_ffn_w_up, L0_ffn_w_down):

    def _L0_attn_a_ref(x, time_mix_k, time_mix_v, time_mix_r, time_decay, time_first, Wk, Wv, Wr, Wo, ln_g, ln_b):
        import jax, jax.numpy as jnp
        import numpy as np
        B, T, C, H = (8, 256, 128, 16)
        S = C // H
        LN_EPS = 1e-05
        Bx, Tx, Cx = x.shape
        xx = jnp.pad(x, ((0, 0), (1, 0), (0, 0)))[:, :-1]
        xk = x * time_mix_k + xx * (1 - time_mix_k)
        xv = x * time_mix_v + xx * (1 - time_mix_v)
        xr = x * time_mix_r + xx * (1 - time_mix_r)
        proj = lambda z, W: jnp.einsum('btc,dc->btd', z, W).reshape(Bx, Tx, H, S)
        k = proj(xk, Wk)
        v = proj(xv, Wv)
        r = proj(xr, Wr)
        kv = k * v
        decay = jnp.exp(time_decay)

        def step(state, inp):
            kv_t, r_t = inp
            state = kv_t + decay * state
            o = r_t * (time_first * kv_t + state)
            return (state, o)
        kvT = jnp.swapaxes(kv, 0, 1)
        rT = jnp.swapaxes(r, 0, 1)
        _, outT = jax.lax.scan(step, jnp.zeros((Bx, H, S), x.dtype), (kvT, rT))
        out = jnp.swapaxes(outT, 0, 1).reshape(Bx, Tx, Cx)
        mu = out.mean(-1, keepdims=True)
        var = out.var(-1, keepdims=True)
        out = (out - mu) / jnp.sqrt(var + LN_EPS) * ln_g + ln_b
        return jnp.einsum('btc,dc->btd', out, Wo)

    def _L0_attn_b_ref(queries, keys, values, attn_mask, mu_r, mu_k, mu_v, mu_g, mu_a, mu_d, dA, dB, db, aA, aB, ab, gA, gB, rW1, rb1, rW2, rb2, kW1, kb1, kW2, kb2, vW1, vb1, vW2, vb2, oW1, ob1, oW2, ob2, rem_mult, iclr_mix, bonus_mult, ln_g, ln_b):
        import jax, jax.numpy as jnp
        import numpy as np
        H_HEADS = 16
        DECAY_C = 0.7408182206817179

        def _gelu(x):
            return jax.nn.gelu(x, approximate=False)

        def _mlp(x, W1, b1, W2, b2):
            return _gelu(x @ W1 + b1) @ W2 + b2

        def _forward(queries, mu_r, mu_k, mu_v, mu_g, mu_a, mu_d, dA, dB, db, aA, aB, ab, gA, gB, rW1, rb1, rW2, rb2, kW1, kb1, kW2, kb2, vW1, vb1, vW2, vb2, oW1, ob1, oW2, ob2, rem_mult, iclr_mix, bonus_mult, ln_g, ln_b):
            B, T, C = queries.shape
            H = H_HEADS
            N = C // H
            r = _mlp(queries + mu_r, rW1, rb1, rW2, rb2)
            k = _mlp(queries + mu_k, kW1, kb1, kW2, kb2)
            v = _mlp(queries + mu_v, vW1, vb1, vW2, vb2)
            gate = jax.nn.sigmoid((queries + mu_g) @ gA @ gB)
            iclr = jax.nn.sigmoid((queries + mu_a) @ aA @ ab + (queries + mu_a) @ aA @ aB) if False else jax.nn.sigmoid((queries + mu_a) @ aA @ aB + ab)
            decay = jnp.exp(-DECAY_C * jax.nn.sigmoid(jnp.tanh((queries + mu_d) @ dA @ dB + db)))
            removal_k = k * rem_mult
            replacement_k = k * (1.0 + (iclr - 1.0) * iclr_mix)
            rh = r.reshape(B, T, H, N)
            rkh = replacement_k.reshape(B, T, H, N)
            vh = v.reshape(B, T, H, N)
            dh = decay.reshape(B, T, H, N)
            ah = iclr.reshape(B, T, H, N)
            rmh = removal_k.reshape(B, T, H, N)
            kn = rmh / jnp.maximum(jnp.linalg.norm(rmh, axis=-1, keepdims=True), 1e-12)
            xs = tuple((jnp.swapaxes(a, 0, 1) for a in (dh, ah, kn, rkh, vh, rh)))

            def step(wkv, x):
                d, a, knt, rk, vt, rt = x
                tmp = jnp.einsum('bhj,bhjk->bhk', a * knt, wkv)
                wkv = d[..., None] * wkv - knt[..., None] * tmp[:, :, None, :] + vt[..., None] * rk[:, :, None, :]
                return (wkv, jnp.einsum('bhij,bhj->bhi', wkv, rt))
            wkv0 = jnp.zeros((B, H, N, N), queries.dtype)
            _, out_t = jax.lax.scan(step, wkv0, xs)
            out = jnp.swapaxes(out_t, 0, 1)
            bonus = jnp.sum(rh * rkh, -1, keepdims=True) * 0.2 * vh * bonus_mult.reshape(1, 1, H, N)
            out = (out + bonus).reshape(B, T, C)
            mu = jnp.mean(out, -1, keepdims=True)
            var = jnp.mean((out - mu) ** 2, -1, keepdims=True)
            out = (out - mu) / jnp.sqrt(var + 1e-06) * ln_g + ln_b
            out = out * gate
            out = _mlp(out, oW1, ob1, oW2, ob2)
            return out
        del keys, values, attn_mask
        return _forward(queries, mu_r, mu_k, mu_v, mu_g, mu_a, mu_d, dA, dB, db, aA, aB, ab, gA, gB, rW1, rb1, rW2, rb2, kW1, kb1, kW2, kb2, vW1, vb1, vW2, vb2, oW1, ob1, oW2, ob2, rem_mult, iclr_mix, bonus_mult, ln_g, ln_b)

    def _L0_ffn_ref(hidden_states, w_router, w_gating, w_gate, w_up, w_down):
        import jax, jax.numpy as jnp
        import numpy as np
        B, S, H = (2, 128, 128)
        E, F = (8, 512)
        GATE_TEMP = 0.1
        x = hidden_states
        router_probs = jax.nn.softmax(jnp.einsum('bsh,he->bse', x, w_router), axis=-1)
        gate_weights = jax.nn.softmax(jnp.einsum('bsh,he->bse', x, w_gating) / GATE_TEMP, axis=-1)
        g = jnp.einsum('bsh,ehf->ebsf', x, w_gate)
        u = jnp.einsum('bsh,ehf->ebsf', x, w_up)
        h = jax.nn.silu(g) * u
        expert_out = jnp.einsum('ebsf,efh->ebsh', h, w_down)
        cw = router_probs * gate_weights
        cw = cw / (jnp.sum(cw, axis=-1, keepdims=True) + 1e-09)
        out = jnp.einsum('ebsh,bse->bsh', expert_out, cw)
        return out
    x = L0_attn_a_x
    x = x + _L0_attn_a_ref(_layernorm(x, axis=-1), L0_attn_a_time_mix_k, L0_attn_a_time_mix_v, L0_attn_a_time_mix_r, L0_attn_a_time_decay, L0_attn_a_time_first, L0_attn_a_Wk, L0_attn_a_Wv, L0_attn_a_Wr, L0_attn_a_Wo, L0_attn_a_ln_g, L0_attn_a_ln_b)
    x = x + _L0_ffn_ref(_layernorm(x, axis=-1), L0_ffn_w_router, L0_ffn_w_gating, L0_ffn_w_gate, L0_ffn_w_up, L0_ffn_w_down)
    x = x + _L0_attn_b_ref(_layernorm(x, axis=-1), L0_attn_b_keys, L0_attn_b_values, L0_attn_b_attn_mask, L0_attn_b_mu_r, L0_attn_b_mu_k, L0_attn_b_mu_v, L0_attn_b_mu_g, L0_attn_b_mu_a, L0_attn_b_mu_d, L0_attn_b_dA, L0_attn_b_dB, L0_attn_b_db, L0_attn_b_aA, L0_attn_b_aB, L0_attn_b_ab, L0_attn_b_gA, L0_attn_b_gB, L0_attn_b_rW1, L0_attn_b_rb1, L0_attn_b_rW2, L0_attn_b_rb2, L0_attn_b_kW1, L0_attn_b_kb1, L0_attn_b_kW2, L0_attn_b_kb2, L0_attn_b_vW1, L0_attn_b_vb1, L0_attn_b_vW2, L0_attn_b_vb2, L0_attn_b_oW1, L0_attn_b_ob1, L0_attn_b_oW2, L0_attn_b_ob2, L0_attn_b_rem_mult, L0_attn_b_iclr_mix, L0_attn_b_bonus_mult, L0_attn_b_ln_g, L0_attn_b_ln_b)
    x = x + _L0_ffn_ref(_layernorm(x, axis=-1), L0_ffn_w_router, L0_ffn_w_gating, L0_ffn_w_gate, L0_ffn_w_up, L0_ffn_w_down)
    return x

_drawn_inputs = setup_inputs


def setup_inputs(seed=0):
    import zlib

    import numpy as np

    out = dict(_drawn_inputs(seed))
    spreads = {'L0_attn_a_ln_g': (1.0, 0.2),
     'L0_attn_a_ln_b': (0.0, 0.1),
     'L0_attn_b_db': (0.0, 2.0),
     'L0_attn_b_ab': (0.0, 2.0),
     'L0_attn_b_rb1': (0.0, 0.8),
     'L0_attn_b_rb2': (0.0, 1.999),
     'L0_attn_b_kb1': (0.0, 0.8),
     'L0_attn_b_kb2': (0.0, 1.382),
     'L0_attn_b_vb1': (0.0, 0.8),
     'L0_attn_b_vb2': (0.0, 1.395),
     'L0_attn_b_ob1': (0.0, 0.624),
     'L0_attn_b_ob2': (0.0, 0.1),
     'L0_attn_b_iclr_mix': (0.699999988079071, 0.6),
     'L0_attn_b_bonus_mult': (1.2000000476837158, 0.6),
     'L0_attn_b_ln_g': (1.0, 0.6),
     'L0_attn_b_ln_b': (0.0, 0.8)}
    factors = {'L0_attn_b_mu_r': 26.439,
     'L0_attn_b_mu_k': 24.107,
     'L0_attn_b_mu_v': 22.881,
     'L0_attn_b_mu_g': 29.584,
     'L0_attn_b_mu_a': 39.639,
     'L0_attn_b_mu_d': 64.0,
     'L0_attn_b_dA': 31.126,
     'L0_attn_b_dB': 30.236,
     'L0_attn_b_aA': 8.0,
     'L0_attn_b_aB': 8.0,
     'L0_attn_b_gA': 8.0,
     'L0_attn_b_gB': 8.0,
     'L0_attn_b_rW1': 8.0,
     'L0_attn_b_rW2': 8.0,
     'L0_attn_b_kW1': 8.0,
     'L0_attn_b_kW2': 8.0,
     'L0_attn_b_vW1': 8.0,
     'L0_attn_b_vW2': 8.0,
     'L0_attn_b_oW1': 3.268,
     'L0_attn_b_rem_mult': 8.0}
    for name, (base, spread) in spreads.items():
        noise = np.random.default_rng([zlib.crc32(name.encode()), seed]).standard_normal(out[name].shape)
        drawn = base * np.exp(spread * noise) if base else spread * noise
        out[name] = jnp.asarray(drawn.astype(out[name].dtype))
    for name, factor in factors.items():
        out[name] = (out[name] * factor).astype(out[name].dtype)
    return out
```

```python
from contextlib import ExitStack

import concourse.bass as bass
from concourse import mybir

F32 = mybir.dt.float32
F32R = mybir.dt.float32r
ALU = mybir.AluOpType
ACT = mybir.ActivationFunctionType
AX_X = mybir.AxisListType.X

P = 128
B, T, C = 2, 1024, 128
H, N = 16, 8
L = B * T // P
G = 4
BLOCKS = L // G
BT = G * P
SECTIONS = B * T // BT
E, F = 8, 512
FC = F // P
CHUNKS = E * FC
EH = 153
ER = EH - P
LOW = 64
DECAY = 0.7408182206817179
LN_EPS = 1e-5
LN_EPS_B = 1e-6

COLS = ["mix_k", "mix_v", "mix_r", "decay", "first", "ln_g", "ln_b",
        "mu_r", "mu_k", "mu_v", "mu_g", "mu_a", "mu_d", "rb1", "kb1", "vb1", "ob1"]
ROWS = ["rem", "mix", "bonus", "ln_g", "ln_b"]


class Count:

    def __init__(self, engine, sem):
        self.engine, self.sem, self.n = engine, sem, 0

    def inc(self, instruction):
        instruction.then_inc(self.sem, 1)
        self.n += 1

    def wait(self):
        self.engine.wait_ge(self.sem, self.n)


FR_LN = 3
FR_Z = 5
FR_HID = {6: (0, 1), 7: (2, 3), 8: (4, 5)}
FR_TOK = {9: (0,), 10: (1,), 11: (2,), 12: (3,)}
FR_SQUASH, FR_LOG, FR_DECAY, FR_SCALE, REC = 13, 13, 14, 15, 16
F1_LN, F1_Z, F1_ROUTE, F1_EXP, F1_CW = 9, 13, 14, 14, 15
BK, BK_Z, BK_HID, BK_OUT, BK_ADD = 3, 14, 15, 16, 17
F2_LN, F2_Z, F2_ROUTE, F2_EXP, F2_CW = 18, 21, 22, 22, 23


def build(nc, a, out):
    ctx = ExitStack()
    with ctx:
        def sb(name, *shape, dtype=F32):
            return ctx.enter_context(nc.sbuf_tensor(name, list(shape), dtype))

        def sem(name):
            return ctx.enter_context(nc.semaphore(name))

        x = sb("x", P, L, C)
        w_hi = sb("w_hi", P, E, 2, F, dtype=F32R)
        w_lo = sb("w_lo", P, E, 2, F, dtype=F32R)
        w_down = sb("w_down", P, E, FC, C)
        w_router = sb("w_router", P, 2 * E)
        ident = sb("ident", P, P)
        ones = sb("ones", P, P)
        neg_half = sb("neg_half", P, 1)
        cols = sb("cols", P, len(COLS))
        rows = sb("rows", P, len(ROWS), C)
        decay_a = sb("decay_a", P, 1)
        w_a = sb("w_a", P, 4, C)
        b_w1 = sb("b_w1", P, 6, P)
        b_w2 = sb("b_w2", P, 4, C)
        b_w2r = sb("b_w2r", P, 3, C)
        b_o2r = sb("b_o2r", P, C)
        b_low = sb("b_low", P, 3, C)
        b_ow1 = sb("b_ow1", P, EH)
        b_row = sb("b_row", 1, 2 * C)
        b_b1r = sb("b_b1r", P, 2)
        b_b1 = sb("b_b1", P, 6)
        stats = sb("stats", P, 2, G, 6)
        mean_var = sb("mean_var", P, 2, G, 2)
        var_eps = sb("var_eps", P, 2, G)
        rstd = sb("rstd", P, 2, G)
        normed = sb("normed", P, 2, G, C)
        zf = sb("zf", P, BT)
        z_hi = sb("z_hi", P, 2, BT, dtype=F32R)
        z_lo = sb("z_lo", P, 2, BT, dtype=F32R)
        probs = sb("probs", P, G * 2, E)
        lmax = sb("lmax", P, G * 2)
        psum_ = sb("psum_", P, G * 2)
        prec = sb("prec", P, G * 2)
        pscale = sb("pscale", P, G)
        cw = sb("cw", P, 2, G, E)
        cwsum = sb("cwsum", P, G)
        sh_buf = sb("sh_buf", P, 6, BT)
        s_buf = sh_buf[:, 0:2, :]
        h_buf = sh_buf[:, 2:6, :]
        rkv = sb("rkv", P, G, 3, C)
        low3 = sb("low3", P, G, 3, C)
        recept, kk, vv = rkv[:, :, 0, :], rkv[:, :, 1, :], rkv[:, :, 2, :]
        td, rate, gate = low3[:, :, 0, :], low3[:, :, 1, :], low3[:, :, 2, :]
        keep = sb("keep", P, 4, G, C)
        local = sb("local", P, G, C)
        cumdec = sb("cumdec", P, G + 1, C)
        trans = sb("trans", P, G, H * N * N)
        zb = sb("zb", P, BT)
        hid = sb("hid", P, 6, BT)
        logdec = sb("logdec", P, G + 1, C)
        invdec = sb("invdec", P, G, C)
        bh = sb("bh", P, G, C)
        kh = sb("kh", P, G, C)
        rem = kh
        scr = sb("scr", P, G, C)
        ss = sb("ss", P, G * H)
        bs = sb("bs", P, G * H)
        locst = sb("locst", P, H * N * N)
        tmp = sb("tmp", P, H, 2 * N)
        readout = sb("readout", P, H * N * N)
        head_mask = sb("head_mask", P, H)
        states = sh_buf[:].rearrange("p a t -> p (a t)")[:, 0:(P + 2) * N].rearrange("p (c k) -> p c k", k=N)

        prod = hid[:, 0:4, :].rearrange("p a b -> p (a b)")
        outer = hid[:, 4:6, :].rearrange("p a b -> p (a b)")
        tr = trans[:].rearrange("p b c -> p (b c)")
        xn = tr[:, 0:B * (T + 1)].rearrange("p (b t) -> p b t", b=B)
        kv = rkv[:].rearrange("p g r c -> p (g r c)")[:, 0:2 * BT].rearrange("p (a t) -> p a t", a=2)
        st_a = low3[:].rearrange("p g r c -> p (g r c)")[:, 0:2 * BT].rearrange("p (a t) -> p a t", a=2)
        oT = keep[:].rearrange("p a g c -> p (a g c)")
        k_sb = scr[:].rearrange("p g c -> p (g c)")
        mixed = hid[:, 0:3, :]
        diff = hid[:, 3:5, :]
        nT = zb[:]
        w0_sb = prod[:, 1024:2048]

        banks = [ctx.enter_context(nc.psum_tensor(f"bank{i}", [P, BT], F32)) for i in range(8)]
        pG, pU, pY, pA, pB = banks[0:2], banks[2:4], banks[4:6], banks[6], banks[7]
        pT = pY[1]

        spill = nc.dram_tensor("trans_spill", (L, P, H * N * N), F32).ap()
        spill4 = nc.dram_tensor("keep_spill", (BLOCKS, 4, P, G, C), F32).ap()

        S = {n: sem(n) for n in (
            "x_in w_in_a w_in_f w_in_b const dve_step pool_step act_step "
            "w_high w_split ln_mv ln_rstd ln_norm ln_T ln_out z_low "
            "mixed_rdy kvr_full k_copied kvr_used decay_rdy ot_full inner_read wo_full x1_rdy "
            "ones_rdy bias_full bias_rdy rl_full rl_used probs_rdy cw_rdy "
            "g_full u_full silu_done h_done d_done y_full y_used "
            "hid_full hid_rdy tokA_full tokB_full tokA_used tokB_used squashed ew_log ew_exp "
            "front_rdy outer_rdy tmp_rdy trans_rdy step_upd readout_rdy readout_used block_done kept "
            "fin_rdy pt_full lt_full lt_copied states_zero bd_rdy start_rdy w0_full w0_rdy trans_in keep_in "
            "back_read o_hid_full o_hid_rdy o_full x3_rdy stored").split()}
        raw_in = [sem(f"raw_in{i}") for i in range(6)]
        spilled = [sem(f"spilled{i}") for i in range(G)]
        st_full = [sem(f"st_full{b}") for b in range(B)]
        st_rdy = [sem(f"st_rdy{b}") for b in range(B)]
        block = ctx.enter_context(nc.Block())

        def vec(h):
            return h.rearrange("(o c) -> o c", o=1)

        FFN_LN = [8, 9, 11, 13, 17, 19, 21, 23]
        FRONT_LN = [10, 12, 14, 15]
        BACK_LN = [16, 18, 20, 22]
        LAG = 2
        STARTS = (0, BLOCKS)
        nch = P // B
        PIECE = nch // 8

        def col(name):
            i = COLS.index(name)
            return cols[:, i:i + 1]

        def row(name, g=G):
            i = ROWS.index(name)
            return rows[:, i:i + 1, :].broadcast_to((P, g, C))

        def flat(v):
            return v.rearrange("p g c -> p (g c)")

        def over_i(v):
            return v.rearrange("p (h k) -> p h k", h=H).unsqueeze(2).broadcast_to((P, H, N, N))

        @block.sync
        def _(sp):
            sp.dma_start(x[:], a["x"].rearrange("b (p i) c -> (b p) i c", i=L)).then_inc(S["x_in"], 16)
            sp.dma_start(cols[:], a["cols"]).then_inc(S["w_in_a"], 16)
            for i, n in enumerate(["Wk", "Wv", "Wr", "Wo"]):
                sp.dma_start(w_a[:, i, :], a[n]).then_inc(S["w_in_a"], 16)

            def load_raw(i):
                if i >= 6:
                    sp.wait_ge(S["w_split"], i - 5)
                sp.dma_start(sh_buf[:, i % 6, :], a[("w_gate", "w_up")[i % 2]][i // 2]).then_inc(raw_in[i % 6], 16)

            for i in range(6):
                load_raw(i)
            sp.dma_start(w_router[:, 0:E], a["w_router"]).then_inc(S["w_in_f"], 16)
            sp.dma_start(w_router[:, E:2 * E], a["w_gating"]).then_inc(S["w_in_f"], 16)
            sp.dma_start(w_down[:], a["w_down"].rearrange("e (f p) h -> p e f h", p=P)).then_inc(S["w_in_f"], 16)
            sp.wait_ge(S["ones_rdy"], 1)
            for i, n in enumerate("rkv"):
                sp.dma_start(b_w1[:, i, :], a[n + "W1"][:, 0:P]).then_inc(S["w_in_b"], 16)
                sp.dma_start(b_w1[:, 3, 32 * i:32 * i + ER], a[n + "W1"][:, P:EH]).then_inc(S["w_in_b"], 16)
                sp.dma_start(b_w2[:, i, :], a[n + "W2"][0:P, :]).then_inc(S["w_in_b"], 16)
                sp.dma_start(b_w2r[32 * i:32 * i + ER, i, :], a[n + "W2"][P:EH, :]).then_inc(S["w_in_b"], 16)
                sp.dma_start(b_w2r[32 * i + ER:32 * i + ER + 1, i, :], vec(a[n + "b2"])).then_inc(S["w_in_b"], 16)
                sp.dma_start(b_b1r[32 * i:32 * i + ER, 0:1], a[n + "b1"][P:EH].rearrange("(c o) -> c o", o=1)).then_inc(S["w_in_b"], 16)
            sp.dma_start(b_b1r[0:ER, 1:2], a["ob1"][P:EH].rearrange("(c o) -> c o", o=1)).then_inc(S["w_in_b"], 16)
            sp.dma_start(b_w1[:, 4, 0:LOW], a["dA"]).then_inc(S["w_in_b"], 16)
            sp.dma_start(b_w1[:, 4, LOW:P], a["aA"]).then_inc(S["w_in_b"], 16)
            sp.dma_start(b_w1[:, 5, 0:LOW], a["gA"]).then_inc(S["w_in_b"], 16)
            sp.dma_start(b_low[0:LOW, 0, :], a["dB"]).then_inc(S["w_in_b"], 16)
            sp.dma_start(b_low[LOW:P, 1, :], a["aB"]).then_inc(S["w_in_b"], 16)
            sp.dma_start(b_low[0:LOW, 2, :], a["gB"]).then_inc(S["w_in_b"], 16)
            sp.dma_start(b_row[0:1, 0:C], vec(a["db"])).then_inc(S["w_in_b"], 16)
            sp.dma_start(b_row[0:1, C:2 * C], vec(a["ab"])).then_inc(S["w_in_b"], 16)
            sp.dma_start(b_ow1[:], a["oW1"]).then_inc(S["w_in_b"], 16)
            sp.dma_start(b_w2[:, 3, :], a["oW2"][0:P, :]).then_inc(S["w_in_b"], 16)
            sp.dma_start(b_o2r[0:ER, :], a["oW2"][P:EH, :]).then_inc(S["w_in_b"], 16)
            sp.dma_start(b_o2r[ER:ER + 1, :], vec(a["ob2"])).then_inc(S["w_in_b"], 16)
            for i in range(len(ROWS)):
                sp.dma_start(rows[:, i, :], a["rows"][i:i + 1, :].broadcast_to((P, C))).then_inc(S["w_in_b"], 16)
            for i in range(6, 2 * E):
                load_raw(i)
            for j in range(BLOCKS):
                for i in range(G):
                    t = G * j + i
                    sp.wait_ge(S["trans_rdy"], t + 1)
                    sp.dma_start(spill[t], trans[:, i, :]).then_inc(spilled[i], 16)
                sp.wait_ge(S["block_done"], j + 1)
                for n, part in enumerate((recept, gate, local[:], cumdec[:, 1:G + 1, :])):
                    sp.dma_start(spill4[j, n], part).then_inc(S["kept"], 16)
            sp.wait_ge(S["kept"], 64 * BLOCKS)
            for b in range(B):
                sp.wait_ge(st_rdy[b], nch)
            for j in range(BLOCKS):
                if j >= 1:
                    sp.wait_ge(S["back_read"], j)
                sp.dma_start(trans[:], spill[G * j:G * j + G].rearrange("g p n -> p g n")).then_inc(S["trans_in"], 16)
                sp.dma_start(keep[:], spill4[j].rearrange("n p g c -> p n g c")).then_inc(S["keep_in"], 16)
            for j in range(BLOCKS):
                sp.wait_ge(S["y_used"], E * (BLOCKS + j + 1))
                sp.dma_start(out.rearrange("b (p i) c -> (b p) i c", i=L)[:, G * j:G * j + G, :],
                             x[:, G * j:G * j + G, :]).then_inc(S["stored"], 16)
            sp.wait_ge(S["stored"], 16 * BLOCKS)

        @block.gpsimd
        def _(pool):
            step = Count(pool, S["pool_step"])
            pool.memset(b_w2r[:], 0.0)
            pool.memset(b_w1[:, 3, :], 0.0)
            pool.memset(b_low[:], 0.0)
            pool.memset(b_w1[:, 5, :], 0.0)
            pool.memset(b_b1r[:], 0.0).then_inc(S["ones_rdy"], 1)
            step.inc(pool.memset(ident[:], 0.0))
            step.inc(pool.memset(ones[:], 1.0))
            step.inc(pool.memset(neg_half[:], -0.5))
            step.wait()
            step.inc(pool.affine_select(out=ident[:], in_=ident[:], compare_op=ALU.not_equal, fill=1.0,
                                        base=0, pattern=[[-1, P]], channel_multiplier=1))
            step.inc(pool.affine_select(out=head_mask[:], in_=ones[:, 0:H], compare_op=ALU.is_ge, fill=0.0,
                                        base=0, pattern=[[-N, H]], channel_multiplier=1))
            step.wait()
            pool.affine_select(out=head_mask[:], in_=head_mask[:], compare_op=ALU.is_ge, fill=0.0,
                               base=N - 1, pattern=[[N, H]], channel_multiplier=-1).then_inc(S["const"], 1)
            pool.memset(xn[:, :, 0:1], 0.0).then_inc(S["const"], 1)

            def ln_rstd(n, eps):
                pool.wait_ge(S["ln_mv"], n + 1)
                step.inc(pool.tensor_scalar(var_eps[:, n % 2, :], mean_var[:, n % 2, :, 1], eps, None, ALU.add))
                step.wait()
                pool.tensor_tensor(rstd[:, n % 2, :], var_eps[:, n % 2, :],
                                   neg_half[:].broadcast_to((P, G)), ALU.pow).then_inc(S["ln_rstd"], 1)

            for n in range(4):
                ln_rstd(n, LN_EPS)
            for i in range(2 * E):
                pool.wait_ge(S["w_high"], i + 1)
                pool.tensor_tensor(w_lo[:, i // 2, i % 2, :], sh_buf[:, i % 6, :], w_hi[:, i // 2, i % 2, :].bitcast(F32),
                                   ALU.subtract).then_inc(S["w_split"], 1)
            for n in range(4, 8):
                ln_rstd(n, LN_EPS)

            def z_low(q):
                pool.wait_ge(S["ln_out"], FFN_LN[q] + 1)
                if q >= 2:
                    pool.wait_ge(S["u_full"], CHUNKS * (q - 1))
                pool.tensor_tensor(z_lo[:, q % 2, :], zf[:], z_hi[:, q % 2, :].bitcast(F32), ALU.subtract).then_inc(S["z_low"], 1)

            def outer_product(j, i):
                t = G * j + i
                pool.wait_ge(S["front_rdy"], j + 1)
                if i == 0:
                    pool.wait_ge(S["tokB_full"], G * (j + 1))
                if t >= 1:
                    pool.wait_ge(S["step_upd"], t)
                pool.tensor_tensor(outer.rearrange("p (h i k) -> p h i k", h=H, i=N),
                                   vv[:, i, :].rearrange("p (h i) -> p h i", h=H).unsqueeze(3).broadcast_to((P, H, N, N)),
                                   over_i(kk[:, i, :]), ALU.mult).then_inc(S["outer_rdy"], 1)

            def transition_step(j, i):
                t = G * j + i
                pool.wait_ge(S["tmp_rdy"], t + 1)
                part = prod.rearrange("p (h i c) -> p h i c", h=H, i=N)[:, :, :, N:2 * N]
                step.inc(pool.tensor_tensor(part, kh[:, i, :].rearrange("p (h i) -> p h i", h=H).unsqueeze(3).broadcast_to((P, H, N, N)),
                                            tmp[:, :, N:2 * N].unsqueeze(2).broadcast_to((P, H, N, N)), ALU.mult))
                step.wait()
                if j >= 1:
                    pool.wait_ge(spilled[i], 16 * j)
                pool.tensor_tensor(trans[:, i, :].rearrange("p (hi k) -> p hi k", k=N),
                                   trans[:, (i - 1) % G, :].rearrange("p (hi k) -> p hi k", k=N),
                                   prod.rearrange("p (hi c) -> p hi c", c=2 * N)[:, :, N:2 * N],
                                   ALU.subtract).then_inc(S["trans_rdy"], 1)

            def read_state(j, i):
                t = G * j + i
                pool.wait_ge(S["step_upd"], t + 1)
                if t >= 1:
                    pool.wait_ge(S["readout_used"], t)
                pool.tensor_tensor(readout[:].rearrange("p (h i k) -> p h i k", h=H, i=N),
                                   locst[:].rearrange("p (h i k) -> p h i k", h=H, i=N),
                                   over_i(recept[:, i, :]), ALU.mult).then_inc(S["readout_rdy"], 1)

            def recurrence(j):
                outer_product(j, 0)
                for i in range(G):
                    transition_step(j, i)
                    read_state(j, i)
                    if i + 1 < G:
                        outer_product(j, i + 1)

            ln_rstd(FFN_LN[0], LN_EPS)
            z_low(0)
            for q in range(BLOCKS):
                if q >= 1:
                    ln_rstd(FRONT_LN[q - 1], LN_EPS)
                if q + 1 < BLOCKS:
                    ln_rstd(FFN_LN[q + 1], LN_EPS)
                    z_low(q + 1)
                if q >= 1:
                    recurrence(q - 1)
            ln_rstd(FRONT_LN[BLOCKS - 1], LN_EPS)
            recurrence(BLOCKS - 1)
            for j in range(BLOCKS):
                ln_rstd(BACK_LN[j], LN_EPS_B)
                ln_rstd(FFN_LN[BLOCKS + j], LN_EPS)
                z_low(BLOCKS + j)

        @block.scalar
        def _(act):
            step = Count(act, S["act_step"])

            def split_high(i):
                act.wait_ge(raw_in[i % 6], 16 * (i // 6 + 1))
                act.activation(w_hi[:, i // 2, i % 2, :], sh_buf[:, i % 6, :], ACT.Copy).then_inc(S["w_high"], 1)

            act.wait_ge(S["w_in_a"], 16 * 5)
            act.activation(decay_a[:], col("decay"), ACT.Exp).then_inc(S["decay_rdy"], 1)
            act.wait_ge(S["const"], 2)
            for g in range(4):
                act.wait_ge(S["ln_T"], g + 1)
                for b in range(B):
                    dst = xn[:, b, 1:1 + T].rearrange("c (p i) -> c i p", i=L)[:, G * g:G * g + G, :]
                    src = pT[:].rearrange("c (i p) -> c i p", i=G)[:, :, b * nch:(b + 1) * nch]
                    ins = act.activation(dst, src, ACT.Copy)
                    if b < B - 1:
                        step.inc(ins)
                ins.then_inc(S["ln_out"], 1)
            for s in range(SECTIONS):
                act.wait_ge(S["kvr_full"], s + 1)
                act.activation(k_sb, pG[0][:], ACT.Copy).then_inc(S["k_copied"], 1)
                for i in range(4 * s, 4 * s + 4):
                    split_high(i)
            for g in range(4):
                act.wait_ge(S["ln_T"], 5 + g)
                if g >= 1:
                    act.wait_ge(S["wo_full"], g)
                act.activation(nT, pT[:], ACT.Identity, scale=col("ln_g"), bias=col("ln_b")).then_inc(S["ln_out"], 1)

            def ffn_z(q):
                act.wait_ge(S["ln_T"], FFN_LN[q] + 1)
                if q >= 1:
                    act.wait_ge(S["rl_full"], q)
                    act.wait_ge(S["z_low"], q)
                step.inc(act.activation(zf[:], pA[:], ACT.Copy))
                if q >= 2:
                    act.wait_ge(S["u_full"], CHUNKS * (q - 1))
                act.activation(z_hi[:, q % 2, :], pA[:], ACT.Copy).then_inc(S["ln_out"], 1)

            def ffn_exp(q):
                act.wait_ge(S["rl_used"], q + 1)
                pr = probs[:].rearrange("p (g s) e -> p g s e", s=2)
                act.activation(pr[:, :, 0, :], pr[:, :, 0, :], ACT.Exp).then_inc(S["probs_rdy"], 1)
                act.activation(pr[:, :, 1, :], pr[:, :, 1, :], ACT.Exp, scale=10.0).then_inc(S["probs_rdy"], 1)

            def silu(q, c):
                m = CHUNKS * q + c
                act.wait_ge(S["g_full"], m + 1)
                if m >= 2:
                    act.wait_ge(S["h_done"], m - 1)
                act.activation(s_buf[:, m % 2, :], pG[m % 2][:], ACT.Silu).then_inc(S["silu_done"], 1)

            def front_z(j):
                act.wait_ge(S["ln_T"], FRONT_LN[j] + 1)
                if j >= 1:
                    act.wait_ge(S["block_done"], j)
                    act.wait_ge(S["kept"], 64 * j)
                act.activation(zb[:], pA[:], ACT.Copy).then_inc(S["ln_out"], 1)
                if j == 0:
                    act.wait_ge(S["bias_rdy"], 1)
                step.inc(act.activation(hid[0:96, 3, :], ones[0:96, 0:1].broadcast_to((96, BT)), ACT.Copy))

            def front_hidden(j, k):
                act.wait_ge(S["hid_full"], 6 * j + k + 1)
                src = (pA, pB)[k % 2]
                if k == 3:
                    step.wait()
                    for r in range(3):
                        ins = act.activation(hid[32 * r:32 * r + ER, k, :], src[32 * r:32 * r + ER, :], ACT.Gelu,
                                             bias=b_b1[32 * r:32 * r + ER, k:k + 1])
                    ins.then_inc(S["hid_rdy"], 1)
                else:
                    m = LOW if k == 5 else P
                    act.activation(hid[0:m, k, :], src[0:m, :], ACT.Gelu if k < 3 else ACT.Identity,
                                   bias=b_b1[0:m, k:k + 1]).then_inc(S["hid_rdy"], 1)

            def front_tokens(j, i):
                t = G * j + i
                act.wait_ge(S["tokA_full"], t + 1)
                act.activation(rkv[:, i].rearrange("p r c -> p (r c)"), pA[:, 0:3 * C], ACT.Copy).then_inc(S["tokA_used"], 1)
                act.wait_ge(S["tokB_full"], t + 1)
                act.activation(low3[:, i].rearrange("p r c -> p (r c)"), pB[:, 0:3 * C], ACT.Copy).then_inc(S["tokB_used"], 1)

            def front_squash(j):
                act.wait_ge(S["tokB_used"], G * (j + 1))
                step.inc(act.activation(td, td, ACT.Tanh))
                step.inc(act.activation(rate, rate, ACT.Tanh, scale=0.5))
                step.inc(act.activation(gate, gate, ACT.Tanh, scale=0.5))
                step.wait()
                act.activation(td, td, ACT.Tanh, scale=0.5).then_inc(S["squashed"], 1)

            def front_decay(j):
                act.wait_ge(S["ew_log"], j + 1)
                act.activation(cumdec[:, 1:G + 1, :], logdec[:, 1:G + 1, :], ACT.Exp, scale=-DECAY / 2).then_inc(S["ew_exp"], 1)
                act.activation(invdec[:], logdec[:, 1:G + 1, :], ACT.Exp, scale=DECAY / 2).then_inc(S["ew_exp"], 1)

            ffn_z(0)
            ffn_exp(0)
            for q in range(BLOCKS):
                j = q - 1
                for c in range(CHUNKS):
                    silu(q, c)
                    if j >= 0:
                        if c == FR_Z:
                            front_z(j)
                        elif c in FR_HID:
                            for k in FR_HID[c]:
                                front_hidden(j, k)
                        elif c in FR_TOK:
                            for i in FR_TOK[c]:
                                front_tokens(j, i)
                        if c == FR_SQUASH:
                            front_squash(j)
                        if c == FR_DECAY:
                            front_decay(j)
                    if q + 1 < BLOCKS:
                        if c == F1_Z:
                            ffn_z(q + 1)
                        elif c == F1_EXP:
                            ffn_exp(q + 1)
            j = BLOCKS - 1
            front_z(j)
            for k in range(6):
                front_hidden(j, k)
            for i in range(G):
                front_tokens(j, i)
            front_squash(j)
            front_decay(j)

            for half, bank in enumerate((pA, pB)):
                act.wait_ge(S["lt_full"], half + 1)
                act.activation(prod[:, 0:1024].rearrange("p (c k) -> p k c", k=N)[:, 4 * half:4 * half + 4, :],
                               bank[:].rearrange("p (k c) -> p k c", k=4), ACT.Copy).then_inc(S["lt_copied"], 1)
            for c in range(nch):
                for b in range(B):
                    act.wait_ge(st_full[b], c + 1)
                    act.activation(states[:, b * (nch + 1) + c + 1, :], pY[b][:, 0:N], ACT.Copy).then_inc(st_rdy[b], 1)
            for half, bank in enumerate((pA, pB)):
                act.wait_ge(S["w0_full"], half + 1)
                act.activation(w0_sb[:, 512 * half:512 * half + 512], bank[:], ACT.Copy).then_inc(S["w0_rdy"], 1)

            def back_z(j):
                act.wait_ge(S["ln_T"], BACK_LN[j] + 1)
                act.activation(zb[:], pA[:], ACT.Copy).then_inc(S["ln_out"], 1)
                step.inc(act.activation(hid[0:32, 5, :], ones[0:32, 0:1].broadcast_to((32, BT)), ACT.Copy))

            def back_hidden(j):
                act.wait_ge(S["o_hid_full"], j + 1)
                step.wait()
                act.activation(hid[:, 4, :], pA[:], ACT.Gelu, bias=col("ob1"))
                act.activation(hid[0:ER, 5, :], pB[0:ER, :], ACT.Gelu, bias=b_b1r[0:ER, 1:2]).then_inc(S["o_hid_rdy"], 1)

            back_z(0)
            back_hidden(0)
            ffn_z(BLOCKS)
            ffn_exp(BLOCKS)
            for q in range(BLOCKS, 2 * BLOCKS):
                j = q - BLOCKS + 1
                for c in range(CHUNKS):
                    silu(q, c)
                    if j < BLOCKS:
                        if c == BK_Z:
                            back_z(j)
                        elif c == BK_HID:
                            back_hidden(j)
                        elif c == F2_Z:
                            ffn_z(q + 1)
                        elif c == F2_EXP:
                            ffn_exp(q + 1)

        @block.tensor
        def _(pe):
            def mm(dst, lhs, rhs, start=True, stop=True, **kw):
                return pe.matmul(dst, lhs, rhs, start=start, stop=stop, **kw)

            free = {}

            def take(bank):
                if bank in free:
                    pe.wait_ge(*free[bank])

            def ln_transposes(n, bank, name):
                pe.wait_ge(S["ln_norm"], n + 1)
                take(name)
                for i in range(G):
                    ins = pe.transpose(bank[:, i * P:(i + 1) * P], normed[:, n % 2, i, :], ident[:])
                ins.then_inc(S["ln_T"], 1)
                free[name] = (S["ln_out"], n + 1)

            pe.wait_ge(S["const"], 1)
            for n in range(4):
                ln_transposes(n, pT, "Y1")
            pe.wait_ge(S["w_in_a"], 16 * 5)
            for s in range(SECTIONS):
                pe.wait_ge(S["mixed_rdy"], s + 1)
                if s >= 1:
                    pe.wait_ge(S["kvr_used"], s)
                for i, bank in enumerate((pG[0], pU[0], pG[1])):
                    ins = mm(bank[:], w_a[:, i, :], mixed[:, i, :])
                ins.then_inc(S["kvr_full"], 1)
            pe.wait_ge(S["kvr_used"], SECTIONS)

            def out_tokens(g):
                if g >= 2:
                    pe.wait_ge(S["inner_read"], g - 1)
                for i in range(G):
                    ins = pe.transpose((pA, pB)[g % 2][:, i * P:(i + 1) * P],
                                       oT.rearrange("c (p i) -> c i p", i=L)[:, G * g + i, :], ident[:])
                ins.then_inc(S["ot_full"], 1)

            out_tokens(0)
            for g in range(4):
                if g + 1 < 4:
                    out_tokens(g + 1)
                ln_transposes(4 + g, pT, "Y1")
                pe.wait_ge(S["ln_out"], 5 + g)
                if g >= 1:
                    pe.wait_ge(S["x1_rdy"], g)
                for i in range(G):
                    ins = mm(pY[0][:, i * P:(i + 1) * P], nT[:, i * P:(i + 1) * P], w_a[:, 3, :])
                ins.then_inc(S["wo_full"], 1)
            pe.wait_ge(S["w_in_b"], 16 * (18 + 1 + 8 + 4 + len(ROWS)))
            for k, mu in enumerate(("mu_r", "mu_k", "mu_v")):
                mm(pG[0][:, k:k + 1], b_w1[:, k, :], col(mu))
            for i, mu in enumerate(("mu_r", "mu_k", "mu_v")):
                mm(pG[0][32 * i:32 * i + 32, 3:4], b_w1[:, 3, 32 * i:32 * i + 32], col(mu))
            mm(pG[0][0:LOW, 4:5], b_w1[:, 4, 0:LOW], col("mu_d"))
            mm(pG[0][LOW:P, 4:5], b_w1[:, 4, LOW:P], col("mu_a"))
            mm(pG[0][0:LOW, 5:6], b_w1[:, 5, 0:LOW], col("mu_g")).then_inc(S["bias_full"], 1)
            pe.wait_ge(S["inner_read"], 4)
            pe.wait_ge(S["w_in_f"], 16 * 3)

            def router(q):
                pe.wait_ge(S["ln_out"], FFN_LN[q] + 1)
                take("B")
                for i in range(G):
                    ins = mm(pB[:, 2 * E * i:2 * E * i + 2 * E], zf[:, i * P:(i + 1) * P], w_router[:])
                ins.then_inc(S["rl_full"], 1)
                free["B"] = (S["rl_used"], q + 1)

            def down(m):
                e, f = divmod(m, FC)
                pe.wait_ge(S["h_done"], m + 1)
                if f == 0 and e >= 2:
                    pe.wait_ge(S["y_used"], e - 1)
                for i in range(G):
                    ins = mm(pY[e % 2][:, i * P:(i + 1) * P], h_buf[:, m % 4, i * P:(i + 1) * P], w_down[:, e % E, f, :],
                             start=(f == 0 and i == 0), stop=(f == FC - 1), skip_group_check=True)
                ins.then_inc(S["y_full" if f == FC - 1 else "d_done"], 1)

            def split_product(bank, lo, hi, z):
                mm(bank, hi, z_lo[:, z, :], stop=False)
                mm(bank, lo, z_hi[:, z, :], start=False, stop=False)
                return mm(bank, hi, z_hi[:, z, :], start=False)

            def chunk(q, c):
                e, f = divmod(c, FC)
                m = CHUNKS * q + c
                cols_f = slice(f * P, (f + 1) * P)
                if m >= 2:
                    pe.wait_ge(S["silu_done"], m - 1)
                split_product(pG[m % 2][:], w_lo[:, e, 0, cols_f], w_hi[:, e, 0, cols_f], q % 2).then_inc(S["g_full"], 1)
                if m >= 2:
                    pe.wait_ge(S["h_done"], m - 1)
                split_product(pU[m % 2][:], w_lo[:, e, 1, cols_f], w_hi[:, e, 1, cols_f], q % 2).then_inc(S["u_full"], 1)
                if c >= LAG or q not in STARTS:
                    down(m - LAG)

            def front_hidden(j, k):
                take("AB"[k % 2])
                m = (P, P, P, 96, P, LOW)[k]
                mm((pA, pB)[k % 2][0:m, :], b_w1[:, k, 0:m], zb[:]).then_inc(S["hid_full"], 1)
                free["AB"[k % 2]] = (S["hid_rdy"], 6 * j + k + 1)

            def front_tokens(j, i):
                t = G * j + i
                tok = slice(i * P, (i + 1) * P)
                pe.wait_ge(S["hid_rdy"], 6 * j + 6)
                take("A")
                mm(pA[:, 0:3 * C], hid[0:96, 3, tok], b_w2r[0:96].rearrange("p r c -> p (r c)"), stop=False)
                for r in range(3):
                    ins = mm(pA[:, r * C:(r + 1) * C], hid[:, r, tok], b_w2[:, r, :], start=False, stop=(r == 2))
                ins.then_inc(S["tokA_full"], 1)
                free["A"] = (S["tokA_used"], t + 1)
                take("B")
                mm(pB[:, 0:2 * C], hid[:, 4, tok], b_low[:, 0:2, :].rearrange("p r c -> p (r c)"), stop=False)
                mm(pB[:, 0:2 * C], ones[0:1, :], b_row[0:1, :], start=False)
                mm(pB[:, 2 * C:3 * C], hid[0:LOW, 5, tok], b_low[0:LOW, 2, :]).then_inc(S["tokB_full"], 1)
                free["B"] = (S["tokB_used"], t + 1)

            ln_transposes(FFN_LN[0], pA, "A")
            router(0)
            pe.wait_ge(S["w_split"], 2 * E)
            pe.wait_ge(S["z_low"], 1)
            pe.wait_ge(S["x1_rdy"], 4)
            pe.wait_ge(S["bias_rdy"], 1)
            for q in range(BLOCKS):
                j = q - 1
                if q >= 1:
                    pe.wait_ge(S["z_low"], q + 1)
                for c in range(CHUNKS):
                    chunk(q, c)
                    if j >= 0:
                        if c == FR_Z:
                            ln_transposes(FRONT_LN[j], pA, "A")
                        elif c in FR_HID:
                            pe.wait_ge(S["ln_out"], FRONT_LN[j] + 1)
                            for k in FR_HID[c]:
                                front_hidden(j, k)
                        elif c in FR_TOK:
                            for i in FR_TOK[c]:
                                front_tokens(j, i)
                    if q + 1 < BLOCKS:
                        if c == F1_Z:
                            ln_transposes(FFN_LN[q + 1], pA, "A")
                        elif c == F1_ROUTE:
                            router(q + 1)
            for m in range(CHUNKS * BLOCKS - LAG, CHUNKS * BLOCKS):
                down(m)
            j = BLOCKS - 1
            ln_transposes(FRONT_LN[j], pA, "A")
            pe.wait_ge(S["ln_out"], FRONT_LN[j] + 1)
            for k in range(6):
                front_hidden(j, k)
            for i in range(G):
                front_tokens(j, i)

            pe.wait_ge(S["fin_rdy"], 2)
            for i in range(N):
                ins = pe.transpose(pG[i // 4][:, (i % 4) * P:(i % 4 + 1) * P], outer[:, i * P:(i + 1) * P], ident[:])
                if i % 4 == 3:
                    ins.then_inc(S["pt_full"], 1)
            lf = locst[:].rearrange("p (hi k) -> p k hi", k=N)
            take("A")
            take("B")
            for k in range(N):
                ins = pe.transpose((pA, pB)[k // 4][:, (k % 4) * P:(k % 4 + 1) * P], lf[:, k], ident[:])
                if k % 4 == 3:
                    ins.then_inc(S["lt_full"], 1)
            pe.wait_ge(S["lt_copied"], 2)
            pe.wait_ge(S["states_zero"], 1)
            pe.wait_ge(S["y_used"], E * BLOCKS)
            bd = tr.rearrange("p (w b c m) -> p w b c m", w=2, b=B, c=PIECE)
            for c in range(nch):
                piece = c // PIECE
                if c % PIECE == 0:
                    pe.wait_ge(S["bd_rdy"], piece + 1)
                for b in range(B):
                    if c >= 1:
                        pe.wait_ge(st_rdy[b], c)
                    cc = b * nch + c
                    mm(pY[b][:, 0:N], ident[:], prod[:, cc * N:cc * N + N], stop=False)
                    mm(pY[b][:, 0:N], bd[:, piece % 2, b, c % PIECE, :], states[:, b * (nch + 1) + c, :],
                       start=False).then_inc(st_full[b], 1)
            pe.wait_ge(S["start_rdy"], 1)
            for k in range(N):
                ins = pe.transpose((pA, pB)[k // 4][:, (k % 4) * P:(k % 4 + 1) * P],
                                   outer[:, k * P:(k + 1) * P], ident[:])
                if k % 4 == 3:
                    ins.then_inc(S["w0_full"], 1)
            free["A"] = free["B"] = (S["w0_rdy"], 2)

            def back_hidden(j):
                pe.wait_ge(S["ln_out"], BACK_LN[j] + 1)
                take("A")
                take("B")
                mm(pA[:], b_ow1[:, 0:P], zb[:])
                mm(pB[0:ER, :], b_ow1[:, P:EH], zb[:]).then_inc(S["o_hid_full"], 1)
                free["A"] = free["B"] = (S["o_hid_rdy"], j + 1)

            def back_out(j):
                take("A")
                for i in range(G):
                    tok = slice(i * P, (i + 1) * P)
                    mm(pA[:, tok], hid[:, 4, tok], b_w2[:, 3, :], stop=False)
                    ins = mm(pA[:, tok], hid[0:ER + 1, 5, tok], b_o2r[0:ER + 1, :], start=False)
                ins.then_inc(S["o_full"], 1)
                free["A"] = (S["x3_rdy"], j + 1)

            ln_transposes(BACK_LN[0], pA, "A")
            back_hidden(0)
            back_out(0)
            ln_transposes(FFN_LN[BLOCKS], pA, "A")
            router(BLOCKS)
            for q in range(BLOCKS, 2 * BLOCKS):
                j = q - BLOCKS + 1
                pe.wait_ge(S["z_low"], q + 1)
                for c in range(CHUNKS):
                    chunk(q, c)
                    if j < BLOCKS:
                        if c == BK_Z:
                            ln_transposes(BACK_LN[j], pA, "A")
                        elif c == BK_HID:
                            back_hidden(j)
                        elif c == BK_OUT:
                            back_out(j)
                        elif c == F2_Z:
                            ln_transposes(FFN_LN[q + 1], pA, "A")
                        elif c == F2_ROUTE:
                            router(q + 1)
            for m in range(2 * CHUNKS * BLOCKS - LAG, 2 * CHUNKS * BLOCKS):
                down(m)

        @block.vector
        def _(dve):
            step = Count(dve, S["dve_step"])

            def ln_stats(n, tiles):
                if n >= 2:
                    dve.wait_ge(S["ln_T"], n - 1)
                for i in range(G):
                    step.inc(dve.bn_stats(stats[:, n % 2, i, :], tiles[:, i, :]))
                step.wait()
                for i in range(G):
                    ins = dve.bn_aggr(mean_var[:, n % 2, i, :], stats[:, n % 2, i, :])
                    if i < G - 1:
                        step.inc(ins)
                ins.then_inc(S["ln_mv"], 1)

            def ln_normalise(n, tiles, last_sem="ln_norm"):
                dve.wait_ge(S["ln_rstd"], n + 1)
                for i in range(G):
                    ins = dve.tensor_scalar(normed[:, n % 2, i, :], tiles[:, i, :], mean_var[:, n % 2, i, 0:1],
                                            rstd[:, n % 2, i:i + 1], ALU.subtract, ALU.mult)
                    if i < G - 1 or not last_sem:
                        step.inc(ins)
                if last_sem:
                    ins.then_inc(S[last_sem], 1)

            def xt(j):
                return x[:, G * j:G * j + G, :]

            dve.wait_ge(S["x_in"], 16)
            ln_stats(0, xt(0))
            for g in range(4):
                if g + 1 < 4:
                    ln_stats(g + 1, xt(g + 1))
                ln_normalise(g, xt(g))
            dve.wait_ge(S["ln_out"], 4)
            dve.wait_ge(S["w_in_a"], 16 * 5)
            dve.wait_ge(S["decay_rdy"], 1)

            def mix(s):
                b, o = s // 2, (s % 2) * BT
                cur, prev = xn[:, b, 1 + o:1 + o + BT], xn[:, b, o:o + BT]
                step.inc(dve.tensor_tensor(diff[:, s % 2, :], cur, prev, ALU.subtract))
                step.wait()
                if s >= 1:
                    dve.wait_ge(S["kvr_full"], s)
                for i, nm in enumerate(("mix_k", "mix_v", "mix_r")):
                    ins = dve.scalar_tensor_tensor(out=mixed[:, i, :], in0=diff[:, s % 2, :], scalar=col(nm), in1=prev,
                                                   op0=ALU.mult, op1=ALU.add)
                    if i < 2:
                        step.inc(ins)
                ins.then_inc(S["mixed_rdy"], 1)

            mix(0)
            for s in range(SECTIONS):
                if s + 1 < SECTIONS:
                    mix(s + 1)
                dve.wait_ge(S["k_copied"], s + 1)
                step.inc(dve.tensor_tensor(kv[:, s % 2, :], k_sb, pU[0][:], ALU.mult))
                step.wait()
                init = 0.0 if s % 2 == 0 else st_a[:, (s - 1) % 2, BT - 1:BT]
                step.inc(dve.tensor_tensor_scan(st_a[:, s % 2, :], decay_a[:].broadcast_to((P, BT)), kv[:, s % 2, :],
                                                init, ALU.mult, ALU.add))
                step.wait()
                step.inc(dve.scalar_tensor_tensor(out=diff[:, s % 2, :], in0=kv[:, s % 2, :], scalar=col("first"),
                                                  in1=st_a[:, s % 2, :], op0=ALU.mult, op1=ALU.add))
                step.wait()
                dve.tensor_tensor(oT[:, s * BT:(s + 1) * BT], diff[:, s % 2, :], pG[1][:],
                                  ALU.mult).then_inc(S["kvr_used"], 1)
                dve.wait_ge(S["kvr_used"], s + 1)

            def inner(g):
                return (pA, pB)[g % 2][:].rearrange("p (i c) -> p i c", i=G)

            dve.wait_ge(S["ot_full"], 1)
            ln_stats(4, inner(0))
            for g in range(4):
                if g + 1 < 4:
                    dve.wait_ge(S["ot_full"], g + 2)
                    ln_stats(5 + g, inner(g + 1))
                ln_normalise(4 + g, inner(g), None)
                step.wait()
                dve.tensor_scalar(tmp[:, 0, 0:1], neg_half[:], 1.0, None, ALU.mult).then_inc(S["inner_read"], 1)
                dve.tensor_scalar(tmp[:, 0, 1:2], neg_half[:], 1.0, None, ALU.mult).then_inc(S["ln_norm"], 1)
                dve.wait_ge(S["wo_full"], g + 1)
                dve.tensor_tensor(xt(g), xt(g), pY[0][:].rearrange("p (i c) -> p i c", i=G), ALU.add).then_inc(S["x1_rdy"], 1)

            def softmax_logits(q):
                lg = pB[:, 0:G * 2 * E].rearrange("p (g e) -> p g e", e=E)
                dve.wait_ge(S["rl_full"], q + 1)
                step.inc(dve.tensor_reduce(lmax[:], lg, AX_X, ALU.max))
                step.wait()
                dve.tensor_tensor(probs[:], lg, lmax[:].unsqueeze(2).broadcast_to((P, 2 * G, E)),
                                  ALU.subtract).then_inc(S["rl_used"], 1)

            def combine_weights(q):
                w = cw[:, q % 2]
                dve.wait_ge(S["probs_rdy"], 2 * q + 2)
                pr = probs[:].rearrange("p (g s) e -> p g s e", s=2)
                step.inc(dve.tensor_reduce(psum_[:], probs[:], AX_X, ALU.add))
                step.inc(dve.tensor_tensor(w, pr[:, :, 0, :], pr[:, :, 1, :], ALU.mult))
                step.wait()
                step.inc(dve.reciprocal(prec[:], psum_[:]))
                step.wait()
                pc = prec[:].rearrange("p (g s) -> p g s", s=2)
                step.inc(dve.tensor_tensor(pscale[:], pc[:, :, 0], pc[:, :, 1], ALU.mult))
                step.wait()
                step.inc(dve.tensor_tensor(w, w, pscale[:].unsqueeze(2).broadcast_to((P, G, E)), ALU.mult))
                step.wait()
                step.inc(dve.tensor_reduce(cwsum[:], w, AX_X, ALU.add))
                step.wait()
                step.inc(dve.tensor_scalar(cwsum[:], cwsum[:], 1e-9, None, ALU.add))
                step.wait()
                step.inc(dve.reciprocal(pscale[:], cwsum[:]))
                step.wait()
                dve.tensor_tensor(w, w, pscale[:].unsqueeze(2).broadcast_to((P, G, E)), ALU.mult).then_inc(S["cw_rdy"], 1)

            def hidden(q, c):
                m = CHUNKS * q + c
                dve.wait_ge(S["silu_done"], m + 1)
                dve.wait_ge(S["u_full"], m + 1)
                if m >= 4:
                    done = m - 3
                    if done % FC == 0:
                        dve.wait_ge(S["y_full"], done // FC)
                    else:
                        dve.wait_ge(S["d_done"], (FC - 1) * (done // FC) + done % FC)
                dve.tensor_tensor(h_buf[:, m % 4, :], s_buf[:, m % 2, :], pU[m % 2][:], ALU.mult).then_inc(S["h_done"], 1)

            def add_expert(q, e):
                eg = E * q + e
                j = q % BLOCKS
                dve.wait_ge(S["y_full"], eg + 1)
                if eg >= 1:
                    dve.wait_ge(S["y_used"], eg)
                if e == 0:
                    dve.wait_ge(S["cw_rdy"], q + 1)
                for i in range(G):
                    tile = x[:, G * j + i, :]
                    ins = dve.scalar_tensor_tensor(out=tile, in0=pY[eg % 2][:, i * P:(i + 1) * P], scalar=cw[:, q % 2, i, e:e + 1],
                                                   in1=tile, op0=ALU.mult, op1=ALU.add)
                    if i < G - 1:
                        step.inc(ins)
                ins.then_inc(S["y_used"], 1)

            def by_head(v):
                return v.rearrange("p g (h n) -> p g h n", n=N)

            def spread(v):
                return v.rearrange("p (g h) -> p g h", g=G).unsqueeze(3).broadcast_to((P, G, H, N))

            def front_log(j):
                dve.wait_ge(S["squashed"], j + 1)
                if j >= 1:
                    dve.wait_ge(S["kept"], 64 * j)
                step.inc(dve.tensor_copy(logdec[:, 0, :], logdec[:, G, :]))
                step.inc(dve.tensor_copy(cumdec[:, 0, :], cumdec[:, G, :]))
                for i in range(G):
                    step.wait()
                    ins = dve.scalar_tensor_tensor(out=logdec[:, i + 1, :], in0=td[:, i, :], scalar=1.0,
                                                   in1=logdec[:, i, :], op0=ALU.add, op1=ALU.add)
                    if i < G - 1:
                        step.inc(ins)
                ins.then_inc(S["ew_log"], 1)

            def front_keys(j):
                step.inc(dve.tensor_scalar(rate, rate, 0.5, 0.5, ALU.mult, ALU.add))
                step.inc(dve.tensor_scalar(gate, gate, 0.5, 0.5, ALU.mult, ALU.add))
                step.inc(dve.tensor_tensor(rem[:], kk, row("rem"), ALU.mult))
                step.wait()
                step.inc(dve.tensor_tensor(scr[:], rem[:], rem[:], ALU.mult))
                step.inc(dve.tensor_tensor(bh[:], rem[:], rate, ALU.mult))
                step.wait()
                step.inc(dve.tensor_reduce(ss[:], by_head(scr[:]), AX_X, ALU.add))
                step.inc(dve.scalar_tensor_tensor(out=rate, in0=rate, scalar=-1.0, in1=row("mix"), op0=ALU.add, op1=ALU.mult))
                step.wait()
                step.inc(dve.tensor_scalar(ss[:], ss[:], 1e-24, None, ALU.max))
                step.inc(dve.scalar_tensor_tensor(out=kk, in0=rate, scalar=1.0, in1=kk, op0=ALU.add, op1=ALU.mult))
                step.wait()
                step.inc(dve.reciprocal(ss[:], ss[:]))

            def front_bonus(j):
                step.inc(dve.tensor_tensor(scr[:], recept, kk, ALU.mult))
                step.wait()
                step.inc(dve.tensor_reduce(bs[:], by_head(scr[:]), AX_X, ALU.add))
                step.inc(dve.tensor_tensor(local[:], vv, row("bonus"), ALU.mult))
                step.wait()
                step.inc(dve.tensor_tensor(by_head(local[:]), by_head(local[:]), spread(bs[:]), ALU.mult))

            def front_scale(j):
                dve.wait_ge(S["ew_exp"], 2 * j + 2)
                step.inc(dve.tensor_tensor(bh[:], bh[:], cumdec[:, 0:G, :], ALU.mult))
                step.inc(dve.tensor_tensor(kh[:], rem[:], invdec[:], ALU.mult))
                step.inc(dve.tensor_tensor(vv, vv, invdec[:], ALU.mult))
                step.wait()
                dve.tensor_tensor(by_head(kh[:]), by_head(kh[:]), spread(ss[:]), ALU.mult).then_inc(S["front_rdy"], 1)
                dve.wait_ge(S["front_rdy"], j + 1)

            p3 = prod.rearrange("p (hi c) -> p hi c", c=2 * N)
            loc3 = locst[:].rearrange("p (hi k) -> p hi k", k=N)

            def read_sum(j, i):
                dve.wait_ge(S["readout_rdy"], G * j + i + 1)
                dve.tensor_reduce(scr[:, i, :], readout[:].rearrange("p (hi k) -> p hi k", k=N), AX_X, ALU.add)\
                   .then_inc(S["readout_used"], 1)

            def step_part(j, i, part):
                t = G * j + i
                if part == 0:
                    if t >= 1:
                        dve.wait_ge(S["step_upd"], t)
                        dve.wait_ge(S["trans_rdy"], t)
                    bb = bh[:, i, :].unsqueeze(2).broadcast_to((P, H * N, N))
                    step.inc(dve.tensor_tensor(p3[:, :, 0:N], loc3, bb, ALU.mult))
                    step.inc(dve.tensor_tensor(p3[:, :, N:2 * N], trans[:, (i - 1) % G, :].rearrange("p (hi k) -> p hi k", k=N),
                                               bb, ALU.mult))
                elif part == 1:
                    step.wait()
                    dve.tensor_reduce(tmp[:], prod.rearrange("p (h i c) -> p h c i", h=H, i=N), AX_X, ALU.add)\
                       .then_inc(S["tmp_rdy"], 1)
                elif part == 2:
                    dve.wait_ge(S["tmp_rdy"], t + 1)
                    step.inc(dve.tensor_tensor(prod.rearrange("p (h i c) -> p h i c", h=H, i=N)[:, :, :, 0:N],
                                               kh[:, i, :].rearrange("p (h i) -> p h i", h=H).unsqueeze(3).broadcast_to((P, H, N, N)),
                                               tmp[:, :, 0:N].unsqueeze(2).broadcast_to((P, H, N, N)), ALU.mult))
                    step.wait()
                    if t >= 1:
                        dve.wait_ge(S["readout_rdy"], t)
                    step.inc(dve.tensor_tensor(loc3, loc3, p3[:, :, 0:N], ALU.subtract))
                else:
                    dve.wait_ge(S["outer_rdy"], t + 1)
                    step.wait()
                    dve.tensor_tensor(locst[:], locst[:], outer, ALU.add).then_inc(S["step_upd"], 1)
                    if i >= 1:
                        read_sum(j, i - 1)

            def block_end(j):
                read_sum(j, G - 1)
                dve.wait_ge(S["readout_used"], G * (j + 1))
                step.inc(dve.tensor_tensor(scr[:], scr[:], cumdec[:, 1:G + 1, :], ALU.mult))
                step.wait()
                dve.tensor_tensor(local[:], local[:], scr[:], ALU.add).then_inc(S["block_done"], 1)
                dve.wait_ge(S["block_done"], j + 1)
                dve.wait_ge(S["step_upd"], G * (j + 1))
                dve.wait_ge(S["trans_rdy"], G * (j + 1))

            ln_stats(FFN_LN[0], xt(0))
            ln_normalise(FFN_LN[0], xt(0))
            dve.wait_ge(S["bias_full"], 1)
            for k, nm in enumerate(("rb1", "kb1", "vb1")):
                step.inc(dve.tensor_tensor(b_b1[:, k:k + 1], pG[0][:, k:k + 1], col(nm), ALU.add))
            step.inc(dve.tensor_tensor(b_b1[0:96, 3:4], pG[0][0:96, 3:4], b_b1r[0:96, 0:1], ALU.add))
            step.inc(dve.tensor_copy(b_b1[:, 4:5], pG[0][:, 4:5]))
            step.inc(dve.memset(locst[:], 0.0))
            step.inc(dve.memset(cumdec[:, G, :], 1.0))
            step.inc(dve.memset(logdec[:, G, :], 0.0))
            last = trans[:, G - 1, :].rearrange("p (h ij) -> p h ij", h=H)
            step.inc(dve.memset(last, 0.0))
            step.wait()
            step.inc(dve.memset(last[:, :, 0:N * N:N + 1], 1.0))
            step.inc(dve.tensor_scalar(rows[:, 2, :], rows[:, 2, :], 0.2, None, ALU.mult))
            step.wait()
            dve.tensor_copy(b_b1[0:LOW, 5:6], pG[0][0:LOW, 5:6]).then_inc(S["bias_rdy"], 1)
            softmax_logits(0)
            combine_weights(0)

            for q in range(BLOCKS):
                j = q - 1
                for c in range(CHUNKS):
                    hidden(q, c)
                    if c % FC == 2 and c > 2:
                        add_expert(q, c // FC - 1)
                    if j >= 0:
                        if c == 2:
                            add_expert(j, E - 1)
                        elif c == FR_LN:
                            dve.wait_ge(S["y_used"], E * (j + 1))
                            ln_stats(FRONT_LN[j], xt(j))
                        elif c == FR_LN + 1:
                            ln_normalise(FRONT_LN[j], xt(j))
                        elif c == FR_SQUASH:
                            dve.wait_ge(S["squashed"], j + 1)
                            front_keys(j)
                        elif c == FR_DECAY:
                            front_bonus(j)
                        elif c == FR_SCALE:
                            front_scale(j)
                        elif c >= REC and (c - REC) // 4 < G:
                            step_part(j, (c - REC) // 4, (c - REC) % 4)
                        if c == FR_LOG:
                            front_log(j)
                    if q + 1 < BLOCKS:
                        if c == F1_LN:
                            ln_stats(FFN_LN[q + 1], xt(q + 1))
                        elif c == F1_LN + 1:
                            ln_normalise(FFN_LN[q + 1], xt(q + 1))
                        elif c == F1_ROUTE:
                            softmax_logits(q + 1)
                        elif c == F1_CW:
                            combine_weights(q + 1)
                if j >= 0:
                    block_end(j)
            j = BLOCKS - 1
            add_expert(j, E - 1)
            dve.wait_ge(S["y_used"], E * BLOCKS)
            ln_stats(FRONT_LN[j], xt(j))
            ln_normalise(FRONT_LN[j], xt(j))
            front_log(j)
            front_keys(j)
            front_bonus(j)
            front_scale(j)
            for i in range(G):
                for part in range(4):
                    step_part(j, i, part)
            block_end(j)

            dend = cumdec[:, G, :].unsqueeze(2).broadcast_to((P, C, N))
            tfin = trans[:, G - 1, :].rearrange("p (c k) -> p c k", k=N)
            dve.tensor_tensor(outer.rearrange("p (i h j) -> p h i j", i=N, h=H), tfin.rearrange("p (h i) j -> p h i j", h=H),
                              dend.rearrange("p (h i) j -> p h i j", h=H), ALU.mult).then_inc(S["fin_rdy"], 1)
            lv = locst[:].rearrange("p (c k) -> p c k", k=N)
            dve.tensor_tensor(lv, lv, dend, ALU.mult).then_inc(S["fin_rdy"], 1)
            dve.memset(states, 0.0).then_inc(S["states_zero"], 1)
            dve.wait_ge(S["pt_full"], 2)
            dve.wait_ge(S["fin_rdy"], 2)
            for i in range(G):
                dve.wait_ge(spilled[i], 16 * BLOCKS)
            for piece in range(nch // PIECE):
                if piece >= 2:
                    for b in range(B):
                        dve.wait_ge(st_full[b], PIECE * (piece - 1))
                dst4 = tr.rearrange("p (w b c h i) -> p w b c h i", w=2, b=B, c=PIECE, h=H)
                for b in range(B):
                    for bank in range(2):
                        first = b * nch + PIECE * piece
                        src = pG[bank][:].rearrange("p (i c) -> p c i", i=4)[:, first:first + PIECE, :]
                        ins = dve.tensor_tensor(dst4[:, piece % 2, b, :, :, 4 * bank:4 * bank + 4],
                                                src.unsqueeze(2).broadcast_to((P, PIECE, H, 4)),
                                                head_mask[:].unsqueeze(1).unsqueeze(3).broadcast_to((P, PIECE, H, 4)), ALU.mult)
                        if not (b == B - 1 and bank == 1):
                            step.inc(ins)
                ins.then_inc(S["bd_rdy"], 1)
            for b in range(B):
                dve.wait_ge(st_rdy[b], nch)
            for b in range(B):
                ins = dve.tensor_copy(outer.rearrange("p (k b c) -> p k b c", k=N, b=B)[:, :, b, :],
                                      states.rearrange("p (b c) k -> p b k c", b=B)[:, b, :, 0:nch])
                if b == 0:
                    step.inc(ins)
                    step.wait()
            ins.then_inc(S["start_rdy"], 1)
            dve.wait_ge(S["w0_rdy"], 2)
            w0 = w0_sb.rearrange("p (k h j) -> p h j k", k=N, h=H)
            ta = prod[:, 0:1024]
            ta4 = ta.rearrange("p (h j k) -> p h j k", h=H, j=N)

            def back_part(j, i, part):
                if part == 0:
                    step.inc(dve.tensor_tensor(ta4, w0, over_i(keep[:, 0, i, :]), ALU.mult))
                    step.wait()
                    step.inc(dve.tensor_reduce(bh[:, i, :], ta.rearrange("p (hj k) -> p hj k", k=N), AX_X, ALU.add))
                    step.wait()
                else:
                    step.inc(dve.tensor_tensor(ta4, trans[:, i, :].rearrange("p (h i j) -> p h i j", h=H, i=N),
                                               over_i(bh[:, i, :]), ALU.mult))
                    step.wait()
                    step.inc(dve.tensor_reduce(scr[:, i, :], ta.rearrange("p (hi j) -> p hi j", j=N), AX_X, ALU.add))
                    step.wait()

            def back_sum(j):
                step.inc(dve.tensor_tensor(scr[:], scr[:], keep[:, 3], ALU.mult))
                step.wait()
                step.inc(dve.tensor_tensor(scr[:], scr[:], keep[:, 2], ALU.add))
                step.wait()
                ln_stats(BACK_LN[j], scr[:])

            def back_norm(j):
                n = BACK_LN[j]
                ln_normalise(n, scr[:], None)
                step.wait()
                nm = normed[:, n % 2]
                step.inc(dve.tensor_tensor(nm, nm, row("ln_g"), ALU.mult))
                step.wait()
                step.inc(dve.tensor_tensor(nm, nm, row("ln_b"), ALU.add))
                step.wait()
                dve.tensor_tensor(nm, nm, keep[:, 1], ALU.mult).then_inc(S["ln_norm"], 1)
                dve.wait_ge(S["ln_norm"], n + 1)
                dve.tensor_scalar(tmp[:, 0, 0:1], neg_half[:], 1.0, None, ALU.mult).then_inc(S["back_read"], 1)

            def back_add(j):
                dve.wait_ge(S["o_full"], j + 1)
                dve.tensor_tensor(xt(j), xt(j), pA[:].rearrange("p (i c) -> p i c", i=G), ALU.add).then_inc(S["x3_rdy"], 1)
                dve.wait_ge(S["x3_rdy"], j + 1)

            def arrived(j):
                dve.wait_ge(S["trans_in"], 16 * (j + 1))
                dve.wait_ge(S["keep_in"], 16 * (j + 1))

            arrived(0)
            for i in range(G):
                back_part(0, i, 0)
                back_part(0, i, 1)
            back_sum(0)
            back_norm(0)
            back_add(0)
            ln_stats(FFN_LN[BLOCKS], xt(0))
            ln_normalise(FFN_LN[BLOCKS], xt(0))
            softmax_logits(BLOCKS)
            combine_weights(BLOCKS)
            for q in range(BLOCKS, 2 * BLOCKS):
                j = q - BLOCKS + 1
                for c in range(CHUNKS):
                    hidden(q, c)
                    if c % FC == 2 and c > 2:
                        add_expert(q, c // FC - 1)
                    if c == 2 and q > BLOCKS:
                        add_expert(q - 1, E - 1)
                    if j < BLOCKS:
                        if BK <= c < BK + 2 * G:
                            if c == BK:
                                arrived(j)
                            back_part(j, (c - BK) // 2, (c - BK) % 2)
                        elif c == BK + 2 * G:
                            back_sum(j)
                        elif c == BK + 2 * G + 1:
                            back_norm(j)
                        elif c == BK_ADD:
                            back_add(j)
                        elif c == F2_LN:
                            ln_stats(FFN_LN[q + 1], xt(j))
                        elif c == F2_LN + 1:
                            ln_normalise(FFN_LN[q + 1], xt(j))
                        elif c == F2_ROUTE:
                            softmax_logits(q + 1)
                        elif c == F2_CW:
                            combine_weights(q + 1)
            add_expert(2 * BLOCKS - 1, E - 1)


A, BB, FF = "L0_attn_a_", "L0_attn_b_", "L0_ffn_"


def kernel(**inputs):
    import numpy as np
    import concourse.bacc as bacc
    from concourse.bass_utils import run_bass_kernel_spmd

    g = {k: np.asarray(v) for k, v in inputs.items()}
    col = [g[A + "time_mix_k"].reshape(C), g[A + "time_mix_v"].reshape(C), g[A + "time_mix_r"].reshape(C),
           g[A + "time_decay"].reshape(C), g[A + "time_first"].reshape(C), g[A + "ln_g"], g[A + "ln_b"]]
    col += [g[BB + "mu_" + n] for n in "rkvgad"]
    col += [g[BB + n + "b1"][0:P] for n in "rkvo"]
    arrays = {
        "x": g[A + "x"],
        "cols": np.ascontiguousarray(np.stack(col, axis=1)),
        "rows": np.stack([g[BB + n] for n in ("rem_mult", "iclr_mix", "bonus_mult", "ln_g", "ln_b")]),
    }
    for n in ("Wk", "Wv", "Wr", "Wo"):
        arrays[n] = np.ascontiguousarray(g[A + n].T)
    for n in ("dA", "dB", "db", "aA", "aB", "ab", "gA", "gB"):
        arrays[n] = g[BB + n]
    for n in "rkvo":
        for m in ("W1", "b1", "W2", "b2"):
            arrays[n + m] = g[BB + n + m]
    for n in ("w_router", "w_gating", "w_gate", "w_up", "w_down"):
        arrays[n] = g[FF + n]

    nc = bacc.Bacc("TRN2", target_bir_lowering=False, num_devices=1)
    aps = {n: nc.dram_tensor("in_" + n, v.shape, F32, kind="ExternalInput").ap() for n, v in arrays.items()}
    out = nc.dram_tensor("out", (B, T, C), F32, kind="ExternalOutput").ap()
    build(nc, aps, out)
    r = run_bass_kernel_spmd(nc, [{"in_" + n: v for n, v in arrays.items()}], core_ids=[0])
    return r.results[0]["out"]
```

```python
from contextlib import ExitStack

import concourse.bass as bass
from concourse import mybir

F32 = mybir.dt.float32
F32R = mybir.dt.float32r
ALU = mybir.AluOpType
ACT = mybir.ActivationFunctionType
AX_X = mybir.AxisListType.X

P = 128
B, T, C = 2, 1024, 128
H, N = 16, 8
UNITS = 2
TU = T // UNITS
NCH = P // B
LU = TU // NCH
L = UNITS * LU
G = 4
BLOCKS = L // G
BT = G * P
BU = BLOCKS // UNITS
PIECE = 8
PIECES = NCH // PIECE
LAG = 2
E, F = 8, 512
FC = F // P
CHUNKS = E * FC
EH = 153
ER = EH - P
LOW = 64
DECAY = 0.7408182206817179
LN_EPS = 1e-5
LN_EPS_B = 1e-6

COLS = ["mix_k", "mix_v", "mix_r", "decay", "first", "ln_g", "ln_b",
        "mu_r", "mu_k", "mu_v", "mu_g", "mu_a", "mu_d", "rb1", "kb1", "vb1", "ob1"]
ROWS = ["rem", "mix", "bonus", "ln_g", "ln_b"]


class Count:

    def __init__(self, engine, sem):
        self.engine, self.sem, self.n = engine, sem, 0

    def inc(self, instruction):
        instruction.then_inc(self.sem, 1)
        self.n += 1

    def wait(self):
        self.engine.wait_ge(self.sem, self.n)


PROLOGUE, SIDE, LINKS = [], [[] for _ in range(2 * BLOCKS * CHUNKS)], [[] for _ in range(2 * BLOCKS * CHUNKS)]


PACK = dict(front=(1, 1.5, 2, 12), step=(0.8, 1.4, 1.4, 1), part=(8, 0.7, 2, 0.7), back=(1, 1, 1, 1), ffn=(1, 1, 1, 1), links=((4,), (4,)), late=1)
SECOND = BLOCKS * CHUNKS


def at(g, *tasks):
    SIDE[g].extend(tasks)


def split_weights(first, last):
    return [("split", i) for i in range(first, last)]


def run_on(g, *stages, pack=1, last=len(SIDE) - 1):
    for slots, *tasks in stages:
        at(min(g + int(slots / pack), last), *tasks)
    return g + int(slots / pack) + 1


def splitter(i):
    own = [0 if k < 6 or k % 2 == 0 else 1 for k in range(i + 1)]
    return own[i], own.count(own[i])


def middle(q, g):
    run_on(g, (0, ("mid_T", q)), (1, ("mid_stats", q)), (2, ("mid_norm", q)), (4, ("mid_z", q)), (5, ("mid_out", q)),
           (6, ("mid_add", q)))


def ffn_input(q, g, **how):
    run_on(g, (0, ("ffn_stats", q)), (1, ("ffn_norm", q)), (3, ("ffn_z", q)), (4, ("route", q), ("logits", q)),
           (5, ("combine", q)), **how)


def project(j, g, ahead=0):
    hidden = [(4 + k // 3, ("front_hidden", j, k)) for k in range(6)]
    tokens = [(6 + i // 2, ("front_tokens", j, i)) for i in range(G)]
    return run_on(g, (0 - ahead, ("front_stats", j)), (1 - ahead, ("front_norm", j)), (3 - ahead, ("front_z", j)),
                  *[(n - ahead, t) for n, t in hidden + tokens], (8 - ahead, ("squash", j)), pack=PACK["front"][j])


def advance(j, g):
    g = run_on(g, (0, ("log", j), ("keys", j)), (1, ("decay", j), ("bonus", j)), (2, ("scale", j)), pack=PACK["front"][j])
    steps = [(n, ("step", j, n // 4, n % 4)) for n in range(4 * G)]
    return run_on(g, *steps, (4 * G - 1, ("block_end", j)), pack=PACK["step"][j]) - 1


def front(j, g):
    return advance(j, project(j, g))


def links(u, g, pattern, last):
    at(min(g, last), ("finish", u), ("finish_T", u), ("pieces", u, 0), ("pieces", u, 1))
    h, c = g + 2, 0
    while c < NCH:
        for _ in range(pattern[h % len(pattern)] if h < last else NCH):
            if c < NCH:
                if h < last:
                    LINKS[h].append((u, c))
                else:
                    at(last, ("link", u, c))
                if c % PIECE == PIECE - 1 and c // PIECE + 2 < PIECES:
                    at(min(h, last), ("pieces", u, c // PIECE + 2))
                c += 1
        if c < NCH:
            h += 1
    h = min(h, last)
    at(h, ("starts", u))
    return h


def back(j, g, **last):
    parts = [(0, 0)] + [p for i in range(1, G) for p in ((i, 0), (i - 1, 1))] + [(G - 1, 1)]
    g = run_on(g, *((n, ("back_part", j, i, part)) for n, (i, part) in enumerate(parts)), pack=PACK["part"][j], **last)
    return run_on(g, (0, ("back_stats", j)), (1, ("back_norm", j)), (3, ("back_z", j)), (4, ("back_hidden", j)),
                  (5, ("back_out", j), ("back_add", j)), pack=PACK["back"][j], **last)


def schedule():
    pro = PROLOGUE
    pro += [("in_stats", 0), ("in_stats", 1), ("in_norm", 0), ("in_z", 0), ("in_norm", 1), ("in_z", 1), ("mix", 0)]
    pro += split_weights(0, 2) + [("kvr", 0), ("mix", 1), ("scan", 0)] + split_weights(2, 4) + [("kvr", 1), ("scan", 1)]
    pro += [("mid_T", 0), ("mid_stats", 0)] + split_weights(4, 7) + [("mid_norm", 0)] + split_weights(7, 9)
    pro += [("mid_z", 0)] + split_weights(9, 11) + [("mid_out", 0), ("mid_add", 0), ("ffn_stats", 0)] + split_weights(11, 13)
    pro += [("ffn_norm", 0)] + split_weights(13, 2 * E) + [("ffn_z", 0), ("route", 0), ("logits", 0), ("combine", 0)]
    middle(1, 0)
    ffn_input(1, 7)
    run_on(4, (0, ("in_stats", 2)), (1, ("in_norm", 2), ("in_stats", 3)), (2, ("in_norm", 3)), (3, ("in_z", 2)), (4, ("in_z", 3)))
    run_on(11, (0, ("mix", 2)), (2, ("kvr", 2)), (3, ("mix", 3)), (4, ("scan", 2)), (5, ("kvr", 3)), (6, ("scan", 3)))
    middle(2, 19)
    middle(3, 26)
    at(31, ("biases",))
    g = CHUNKS
    front(0, g + 3)
    ffn_input(2, g + 12)
    g = 2 * CHUNKS
    ffn_input(3, g - 3)
    end = front(1, g + 3)
    end = links(0, end + 1, PACK["links"][0], SECOND - 1)
    project(2, end + 1, ahead=2)
    end = back(0, end + 1, last=SECOND - 1)
    ffn_input(4, end, pack=PACK["ffn"][0], last=SECOND - 1)
    end = back(1, min(end, SECOND))
    at(end, ("restart",))
    ffn_input(5, max(end, SECOND), pack=PACK["ffn"][1])
    end = advance(2, end)
    end = front(3, end - int(3 / PACK["front"][3]))
    last = SECOND + 2 * CHUNKS - 1
    end = links(1, end + 1, PACK["links"][1], last)
    end = back(2, min(end + 1, last), last=last)
    ffn_input(6, end, pack=PACK["ffn"][2], last=last)
    ffn_input(7, back(3, last + PACK["late"]), pack=PACK["ffn"][3])


def all_tasks():
    return PROLOGUE + [t for side in SIDE for t in side]


schedule()


def build(nc, a, out):
    ctx = ExitStack()
    with ctx:
        def sb(name, *shape, dtype=F32):
            return ctx.enter_context(nc.sbuf_tensor(name, list(shape), dtype))

        def sem(name):
            return ctx.enter_context(nc.semaphore(name))

        x = sb("x", P, L, C)
        w_hi = sb("w_hi", P, E, 2, F, dtype=F32R)
        w_lo = sb("w_lo", P, E, 2, F, dtype=F32R)
        w_down = sb("w_down", P, E, FC, C)
        w_router = sb("w_router", P, 2 * E)
        ident = sb("ident", P, P)
        ones = sb("ones", P, P)
        neg_half = sb("neg_half", P, 1)
        cols = sb("cols", P, len(COLS))
        rows = sb("rows", P, len(ROWS), C)
        decay_a = sb("decay_a", P, 1)
        w_a = sb("w_a", P, 4, C)
        b_w1 = sb("b_w1", P, 6, P)
        b_w2 = sb("b_w2", P, 4, C)
        b_w2r = sb("b_w2r", P, 3, C)
        b_o2r = sb("b_o2r", P, C)
        b_low = sb("b_low", P, 3, C)
        b_ow1 = sb("b_ow1", P, EH)
        b_row = sb("b_row", 1, 2 * C)
        b_b1r = sb("b_b1r", P, 2)
        b_b1 = sb("b_b1", P, 6)
        stats = sb("stats", P, 2, G, 6)
        mean_var = sb("mean_var", P, 2, G, 2)
        var_eps = sb("var_eps", P, 2, G)
        rstd = sb("rstd", P, 2, G)
        normed = sb("normed", P, 2, G, C)
        zf = sb("zf", P, BT)
        z_hi = sb("z_hi", P, 2, BT, dtype=F32R)
        z_lo = sb("z_lo", P, 2, BT, dtype=F32R)
        probs = sb("probs", P, G * 2, E)
        lmax = sb("lmax", P, G * 2)
        psum_ = sb("psum_", P, G * 2)
        prec = sb("prec", P, G * 2)
        pscale = sb("pscale", P, G)
        cw = sb("cw", P, 2, G, E)
        cwsum = sb("cwsum", P, G)
        sh_buf = sb("sh_buf", P, 6, BT)
        y_weighted = sb("y_weighted", P, BT)
        s_buf = sh_buf[:, 0:2, :]
        h_buf = sh_buf[:, 2:6, :]
        rkv = sb("rkv", P, G, 3, C)
        low3 = sb("low3", P, G, 3, C)
        recept, kk, vv = rkv[:, :, 0, :], rkv[:, :, 1, :], rkv[:, :, 2, :]
        td, rate, gate = low3[:, :, 0, :], low3[:, :, 1, :], low3[:, :, 2, :]
        keep = sb("keep", P, 4, G, C)
        local = sb("local", P, G, C)
        cumdec = sb("cumdec", P, G + 1, C)
        trans = sb("trans", P, G, H * N * N)
        zb = sb("zb", P, BT)
        hid = sb("hid", P, 6, BT)
        logdec = sb("logdec", P, G + 1, C)
        invdec = sb("invdec", P, G, C)
        bh = sb("bh", P, G, C)
        kh = sb("kh", P, G, C)
        rem = kh
        scr = sb("scr", P, G, C)
        ss = sb("ss", P, G * H)
        bs = sb("bs", P, G * H)
        locst = sb("locst", P, H * N * N)
        tmp = sb("tmp", P, H, 2 * N)
        readout = sb("readout", P, H * N * N)
        head_mask = sb("head_mask", P, H)
        states = readout[:].rearrange("p (c b k) -> p c b k", b=B, k=N)
        last_state = sb("last_state", P, B, N)
        scan_end = sb("scan_end", P, B)

        prod = hid[:, 0:4, :].rearrange("p a b -> p (a b)")
        outer = hid[:, 4:6, :].rearrange("p a b -> p (a b)")
        tr = trans[:].rearrange("p b c -> p (b c)")
        xn = tr[:, 0:B * (T + 1)].rearrange("p (b t) -> p b t", b=B)
        kv = rkv[:].rearrange("p g r c -> p (g r c)")[:, 0:2 * BT].rearrange("p (a t) -> p a t", a=2)
        st_a = low3[:].rearrange("p g r c -> p (g r c)")[:, 0:2 * BT].rearrange("p (a t) -> p a t", a=2)
        oT = keep[:].rearrange("p a g c -> p (a g c)")
        k_sb = scr[:].rearrange("p g c -> p (g c)")
        mixed = hid[:, 0:3, :]
        diff = hid[:, 3:5, :]
        nT = zb[:]
        local_T = prod[:, 0:P * N]
        trans_T = prod[:, P * N:2 * P * N]
        w0_sb = locst[:]
        out_hid = readout[:].rearrange("p (a t) -> p a t", a=2)
        zb_out = bh[:].rearrange("p g c -> p (g c)")

        banks = [ctx.enter_context(nc.psum_tensor(f"bank{i}", [P, BT], F32)) for i in range(8)]
        pG, pU, pY, pA, pB = banks[0:2], banks[2:4], banks[4:6], banks[6], banks[7]
        bank_named = dict(G0=pG[0], G1=pG[1], U0=pU[0], U1=pU[1], Y0=pY[0], Y1=pY[1], A=pA, B=pB)

        spill = nc.dram_tensor("trans_spill", (L, P, H * N * N), F32).ap()
        spill4 = nc.dram_tensor("keep_spill", (BLOCKS, 4, P, G, C), F32).ap()

        S = {n: sem(n) for n in (
            "w_in_a w_in_f w_in_b const dve_step pool_step act_step "
            "w_high ln_mv ln_rstd ln_norm ln_T ln_out z_low "
            "mixed_rdy kv_full kvr_full k_copied kv_read kvr_used decay_rdy ot_full inner_read wo_full x1_rdy "
            "ones_rdy bias_full bias_rdy rl_full rl_used probs_rdy cw_rdy "
            "g_full u_full silu_done h_done d_done y_full "
            "hid_full hid_rdy tokA_full tokB_full tokA_used tokB_used squashed ew_log ew_exp "
            "front_rdy outer_rdy tmp_rdy trans_rdy step_upd readout_rdy readout_used block_done kept "
            "fin_rdy fin_full trans_copied fin_copied first_rdy bd_rdy link_full link_rdy w0_full w0_rdy keep_in "
            "y0_rdy y1_rdy y1_used y_scaled x_added back_read o_hid_full o_hid_rdy o_full x3_rdy stored").split()}
        trans_in = [sem(f"trans_in{i}") for i in range(2)]
        w_split = [sem(n) for n in ("w_split_pool", "w_split_dve")]
        x_in = [sem(f"x_in{u}") for u in range(UNITS)]
        raw_in = [sem(f"raw_in{i}") for i in range(6)]
        spilled = [sem(f"spilled{i}") for i in range(G)]
        block = ctx.enter_context(nc.Block())

        def vec(h):
            return h.rearrange("(o c) -> o c", o=1)

        order = [t for t in all_tasks() if t[0].endswith("_stats")]
        LN = {(t[0][:-6], t[1]): n for n, t in enumerate(order)}

        def bank_name(part, n):
            if part in ("k", "v", "r"):
                return dict(k="G0", v="U0", r="G1")[part] if n < B else dict(k="A", v="B", r="A")[part]
            if part == "in_z":
                return ("Y0", "Y1")[n] if n < BU else "AB"[n % 2]
            if part == "mid_z":
                return "Y1" if n == 0 else "B"
            if part == "mid_out":
                return "Y0" if n == 0 else "A"
            return "A"

        def bank_of(part, n):
            return bank_named[bank_name(part, n)]

        def col(name):
            i = COLS.index(name)
            return cols[:, i:i + 1]

        def row(name, g=G):
            i = ROWS.index(name)
            return rows[:, i:i + 1, :].broadcast_to((P, g, C))

        def flat(v):
            return v.rearrange("p g c -> p (g c)")

        def over_i(v):
            return v.rearrange("p (h k) -> p h k", h=H).unsqueeze(2).broadcast_to((P, H, N, N))

        @block.sync
        def _(sp):
            def rows_of(h, u, b):
                return h[b, u * TU:(u + 1) * TU, :].rearrange("(p i) c -> p i c", i=LU)

            def load_x(u):
                for b in range(B):
                    sp.dma_start(x[b * NCH:(b + 1) * NCH, u * LU:(u + 1) * LU, :], rows_of(a["x"], u, b)).then_inc(x_in[u], 16)

            def load_raw(i):
                if i >= 6:
                    engine, count = splitter(i - 6)
                    sp.wait_ge(w_split[engine], count)
                sp.dma_start(sh_buf[:, i % 6, :], a[("w_gate", "w_up")[i % 2]][i // 2]).then_inc(raw_in[i % 6], 16)

            load_x(0)
            sp.dma_start(cols[:], a["cols"]).then_inc(S["w_in_a"], 16)
            for i, n in enumerate(["Wk", "Wv", "Wr", "Wo"]):
                sp.dma_start(w_a[:, i, :], a[n]).then_inc(S["w_in_a"], 16)
            for i in range(6):
                load_raw(i)
            sp.dma_start(w_router[:, 0:E], a["w_router"]).then_inc(S["w_in_f"], 16)
            sp.dma_start(w_router[:, E:2 * E], a["w_gating"]).then_inc(S["w_in_f"], 16)
            for i in range(6, 2 * E):
                load_raw(i)
            sp.dma_start(w_down[:], a["w_down"].rearrange("e (f p) h -> p e f h", p=P)).then_inc(S["w_in_f"], 16)
            load_x(1)
            sp.wait_ge(S["ones_rdy"], 1)
            for i, n in enumerate("rkv"):
                sp.dma_start(b_w1[:, i, :], a[n + "W1"][:, 0:P]).then_inc(S["w_in_b"], 16)
                sp.dma_start(b_w1[:, 3, 32 * i:32 * i + ER], a[n + "W1"][:, P:EH]).then_inc(S["w_in_b"], 16)
                sp.dma_start(b_w2[:, i, :], a[n + "W2"][0:P, :]).then_inc(S["w_in_b"], 16)
                sp.dma_start(b_w2r[32 * i:32 * i + ER, i, :], a[n + "W2"][P:EH, :]).then_inc(S["w_in_b"], 16)
                sp.dma_start(b_w2r[32 * i + ER:32 * i + ER + 1, i, :], vec(a[n + "b2"])).then_inc(S["w_in_b"], 16)
                sp.dma_start(b_b1r[32 * i:32 * i + ER, 0:1], a[n + "b1"][P:EH].rearrange("(c o) -> c o", o=1)).then_inc(S["w_in_b"], 16)
            sp.dma_start(b_b1r[0:ER, 1:2], a["ob1"][P:EH].rearrange("(c o) -> c o", o=1)).then_inc(S["w_in_b"], 16)
            sp.dma_start(b_w1[:, 4, 0:LOW], a["dA"]).then_inc(S["w_in_b"], 16)
            sp.dma_start(b_w1[:, 4, LOW:P], a["aA"]).then_inc(S["w_in_b"], 16)
            sp.dma_start(b_w1[:, 5, 0:LOW], a["gA"]).then_inc(S["w_in_b"], 16)
            sp.dma_start(b_low[0:LOW, 0, :], a["dB"]).then_inc(S["w_in_b"], 16)
            sp.dma_start(b_low[LOW:P, 1, :], a["aB"]).then_inc(S["w_in_b"], 16)
            sp.dma_start(b_low[0:LOW, 2, :], a["gB"]).then_inc(S["w_in_b"], 16)
            sp.dma_start(b_row[0:1, 0:C], vec(a["db"])).then_inc(S["w_in_b"], 16)
            sp.dma_start(b_row[0:1, C:2 * C], vec(a["ab"])).then_inc(S["w_in_b"], 16)
            sp.dma_start(b_ow1[:], a["oW1"]).then_inc(S["w_in_b"], 16)
            sp.dma_start(b_w2[:, 3, :], a["oW2"][0:P, :]).then_inc(S["w_in_b"], 16)
            sp.dma_start(b_o2r[0:ER, :], a["oW2"][P:EH, :]).then_inc(S["w_in_b"], 16)
            sp.dma_start(b_o2r[ER:ER + 1, :], vec(a["ob2"])).then_inc(S["w_in_b"], 16)
            for i in range(len(ROWS)):
                sp.dma_start(rows[:, i, :], a["rows"][i:i + 1, :].broadcast_to((P, C))).then_inc(S["w_in_b"], 16)

            def spill_block(j):
                for i in range(G):
                    t = G * j + i
                    sp.wait_ge(S["trans_rdy"], t + 1)
                    sp.dma_start(spill[t], trans[:, i, :]).then_inc(spilled[i], 16)
                sp.wait_ge(S["block_done"], j + 1)
                for n, part in enumerate((recept, gate, local[:], cumdec[:, 1:G + 1, :])):
                    sp.dma_start(spill4[j, n], part).then_inc(S["kept"], 16)

            def load_block(j):
                if j % BU == 0:
                    sp.wait_ge(S["kept"], 64 * (j + BU))
                if j >= 1:
                    sp.wait_ge(S["back_read"], j)
                sp.dma_start(keep[:], spill4[j].rearrange("n p g c -> p n g c")).then_inc(S["keep_in"], 16)
                if j % BU == 0:
                    for i in range(G):
                        sp.wait_ge(spilled[i], 16 * (j + BU))
                for half in range(2):
                    if j % BU == 0:
                        sp.wait_ge(S["link_full"], NCH * (j // BU + 1) - PIECE * (1 - half))
                    first = G * j + 2 * half
                    sp.dma_start(trans[:, 2 * half:2 * half + 2, :],
                                 spill[first:first + 2].rearrange("g p n -> p g n")).then_inc(trans_in[half], 16)

            def store_block(j):
                sp.wait_ge(S["x_added"], E * (BLOCKS + j + 1))
                for b in range(B):
                    sp.dma_start(rows_of(out, j // BU, b)[:, G * (j % BU):G * (j % BU) + G, :],
                                 x[b * NCH:(b + 1) * NCH, G * j:G * j + G, :]).then_inc(S["stored"], 16)

            for u in range(UNITS):
                for j in range(BU * u, BU * u + BU):
                    spill_block(j)
                for j in range(BU * u, BU * u + BU):
                    load_block(j)
            for j in range(BLOCKS):
                store_block(j)
            sp.wait_ge(S["stored"], 16 * B * BLOCKS)

        @block.gpsimd
        def _(pool):
            step = Count(pool, S["pool_step"])
            pool.memset(b_w2r[:], 0.0)
            pool.memset(b_w1[:, 3, :], 0.0)
            pool.memset(b_low[:], 0.0)
            pool.memset(b_w1[:, 5, :], 0.0)
            pool.memset(b_b1r[:], 0.0).then_inc(S["ones_rdy"], 1)
            step.inc(pool.memset(ident[:], 0.0))
            step.inc(pool.memset(ones[:], 1.0))
            step.inc(pool.memset(neg_half[:], -0.5))
            step.wait()
            step.inc(pool.affine_select(out=ident[:], in_=ident[:], compare_op=ALU.not_equal, fill=1.0,
                                        base=0, pattern=[[-1, P]], channel_multiplier=1))
            step.inc(pool.affine_select(out=head_mask[:], in_=ones[:, 0:H], compare_op=ALU.is_ge, fill=0.0,
                                        base=0, pattern=[[-N, H]], channel_multiplier=1))
            step.wait()
            pool.affine_select(out=head_mask[:], in_=head_mask[:], compare_op=ALU.is_ge, fill=0.0,
                               base=N - 1, pattern=[[N, H]], channel_multiplier=-1).then_inc(S["const"], 1)
            pool.memset(xn[:, :, 0:1], 0.0).then_inc(S["const"], 1)

            def ln_rstd(n, eps):
                pool.wait_ge(S["ln_mv"], n + 1)
                step.inc(pool.tensor_scalar(var_eps[:, n % 2, :], mean_var[:, n % 2, :, 1], eps, None, ALU.add))
                step.wait()
                pool.tensor_tensor(rstd[:, n % 2, :], var_eps[:, n % 2, :],
                                   neg_half[:].broadcast_to((P, G)), ALU.pow).then_inc(S["ln_rstd"], 1)

            def z_low(q):
                pool.wait_ge(S["ln_out"], LN["ffn", q] + 1)
                if q >= 2:
                    pool.wait_ge(S["u_full"], CHUNKS * (q - 1))
                pool.tensor_tensor(z_lo[:, q % 2, :], zf[:], z_hi[:, q % 2, :].bitcast(F32), ALU.subtract).then_inc(S["z_low"], 1)

            def outer_product(j, i):
                t = G * j + i
                pool.wait_ge(S["front_rdy"], j + 1)
                if i == 0:
                    pool.wait_ge(S["tokB_full"], G * (j + 1))
                if t >= 1:
                    pool.wait_ge(S["step_upd"], t)
                pool.tensor_tensor(outer.rearrange("p (h i k) -> p h i k", h=H, i=N),
                                   vv[:, i, :].rearrange("p (h i) -> p h i", h=H).unsqueeze(3).broadcast_to((P, H, N, N)),
                                   over_i(kk[:, i, :]), ALU.mult).then_inc(S["outer_rdy"], 1)

            def transition_step(j, i):
                t = G * j + i
                pool.wait_ge(S["tmp_rdy"], t + 1)
                part = prod.rearrange("p (h i c) -> p h i c", h=H, i=N)[:, :, :, N:2 * N]
                step.inc(pool.tensor_tensor(part, kh[:, i, :].rearrange("p (h i) -> p h i", h=H).unsqueeze(3).broadcast_to((P, H, N, N)),
                                            tmp[:, :, N:2 * N].unsqueeze(2).broadcast_to((P, H, N, N)), ALU.mult))
                step.wait()
                if j >= 1:
                    pool.wait_ge(spilled[i], 16 * j)
                pool.tensor_tensor(trans[:, i, :].rearrange("p (hi k) -> p hi k", k=N),
                                   trans[:, (i - 1) % G, :].rearrange("p (hi k) -> p hi k", k=N),
                                   prod.rearrange("p (hi c) -> p hi c", c=2 * N)[:, :, N:2 * N],
                                   ALU.subtract).then_inc(S["trans_rdy"], 1)

            def read_state(j, i):
                t = G * j + i
                pool.wait_ge(S["step_upd"], t + 1)
                if t >= 1:
                    pool.wait_ge(S["readout_used"], t)
                pool.tensor_tensor(readout[:].rearrange("p (h i k) -> p h i k", h=H, i=N),
                                   locst[:].rearrange("p (h i k) -> p h i k", h=H, i=N),
                                   over_i(recept[:, i, :]), ALU.mult).then_inc(S["readout_rdy"], 1)

            def pieces(u, piece):
                n = PIECES * u + piece
                pool.wait_ge(S["trans_copied"], u + 1)
                if piece == 0:
                    for i in range(G):
                        pool.wait_ge(spilled[i], 16 * BU * (u + 1))
                if piece >= 2:
                    pool.wait_ge(S["link_full"], NCH * u + PIECE * (piece - 1))
                for b in range(B):
                    src = trans_T.rearrange("p (b c i) -> p b c i", b=B, i=N)[:, b, PIECE * piece:PIECE * piece + PIECE, :]
                    ins = pool.tensor_tensor(tr.rearrange("p (w b c h i) -> p w b c h i", w=2, b=B, c=PIECE, h=H)[:, n % 2, b],
                                             src.unsqueeze(2).broadcast_to((P, PIECE, H, N)),
                                             head_mask[:].unsqueeze(1).unsqueeze(3).broadcast_to((P, PIECE, H, N)), ALU.mult)
                    if b < B - 1:
                        step.inc(ins)
                ins.then_inc(S["bd_rdy"], 1)

            def through_transition(j, i):
                t = G * j + i
                pool.wait_ge(S["y0_rdy"], t + 1)
                pool.wait_ge(trans_in[i // 2], 16 * (j + 1))
                pool.tensor_tensor(trans[:, i, :].rearrange("p (h i j) -> p h i j", h=H, i=N),
                                   trans[:, i, :].rearrange("p (h i j) -> p h i j", h=H, i=N),
                                   over_i(bh[:, i, :]), ALU.mult).then_inc(S["y1_rdy"], 1)

            def add_expert(q, e):
                j = q % BLOCKS
                pool.wait_ge(S["y_scaled"], E * q + e + 1)
                if e == 0 and q < BLOCKS:
                    pool.wait_ge(S["x1_rdy"], q + 1)
                pool.tensor_tensor(flat(x[:, G * j:G * j + G, :]), flat(x[:, G * j:G * j + G, :]), y_weighted[:],
                                   ALU.add).then_inc(S["x_added"], 1)
                pool.wait_ge(S["x_added"], E * q + e + 1)

            def run(task, *n):
                if task == "split":
                    i = n[0]
                    if splitter(i)[0] == 0:
                        pool.wait_ge(S["w_high"], i + 1)
                        pool.tensor_tensor(w_lo[:, i // 2, i % 2, :], sh_buf[:, i % 6, :], w_hi[:, i // 2, i % 2, :].bitcast(F32),
                                           ALU.subtract).then_inc(w_split[0], 1)
                elif task.endswith("_stats"):
                    ln_rstd(LN[task[:-6], n[0]], LN_EPS_B if task == "back_stats" else LN_EPS)
                elif task == "ffn_z":
                    z_low(n[0])
                elif task == "step":
                    j, i, part = n
                    if part == 0:
                        outer_product(j, i)
                    elif part == 1:
                        transition_step(j, i)
                    elif part == 3:
                        read_state(j, i)
                elif task == "pieces":
                    pieces(*n)
                elif task == "back_part" and n[2] == 1:
                    through_transition(*n[:2])

            for t in PROLOGUE:
                run(*t)
            for g in range(len(SIDE)):
                if g > FC and g % FC == 3:
                    add_expert(*divmod(g // FC - 1, E))
                for t in SIDE[g]:
                    run(*t)
            add_expert(2 * BLOCKS - 1, E - 1)

        @block.scalar
        def _(act):
            step = Count(act, S["act_step"])

            free = {}

            def setup():
                act.wait_ge(S["w_in_a"], 16 * 5)
                act.activation(decay_a[:], col("decay"), ACT.Exp).then_inc(S["decay_rdy"], 1)
                act.wait_ge(S["const"], 2)

            def in_z(q):
                u, g = divmod(q, BU)
                act.wait_ge(S["ln_T"], LN["in", q] + 1)
                for b in range(B):
                    dst = xn[:, b, 1 + u * TU:1 + (u + 1) * TU].rearrange("c (p i) -> c i p", i=LU)[:, G * g:G * g + G, :]
                    src = bank_of("in_z", q)[:].rearrange("c (i p) -> c i p", i=G)[:, :, b * NCH:(b + 1) * NCH]
                    ins = act.activation(dst, src, ACT.Copy)
                    if b < B - 1:
                        step.inc(ins)
                ins.then_inc(S["ln_out"], 1)

            def copy_k(s):
                act.wait_ge(S["kv_full"], s + 1)
                if s >= 1:
                    act.wait_ge(S["kv_read"], s)
                act.activation(k_sb, bank_of("k", s)[:], ACT.Copy).then_inc(S["k_copied"], 1)

            def mid_z(q):
                act.wait_ge(S["ln_T"], LN["mid", q] + 1)
                if q >= 1:
                    act.wait_ge(S["wo_full"], q)
                act.activation(nT, bank_of("mid_z", q)[:], ACT.Identity, scale=col("ln_g"), bias=col("ln_b")).then_inc(S["ln_out"], 1)

            def split_high(i):
                act.wait_ge(raw_in[i % 6], 16 * (i // 6 + 1))
                act.activation(w_hi[:, i // 2, i % 2, :], sh_buf[:, i % 6, :], ACT.Copy).then_inc(S["w_high"], 1)

            def ffn_z(q):
                act.wait_ge(S["ln_T"], LN["ffn", q] + 1)
                if q >= 1:
                    act.wait_ge(S["rl_full"], q)
                    act.wait_ge(S["z_low"], q)
                step.inc(act.activation(zf[:], pA[:], ACT.Copy))
                if q >= 2:
                    act.wait_ge(S["u_full"], CHUNKS * (q - 1))
                act.activation(z_hi[:, q % 2, :], pA[:], ACT.Copy).then_inc(S["ln_out"], 1)

            def ffn_exp(q):
                act.wait_ge(S["rl_used"], q + 1)
                pr = probs[:].rearrange("p (g s) e -> p g s e", s=2)
                act.activation(pr[:, :, 0, :], pr[:, :, 0, :], ACT.Exp).then_inc(S["probs_rdy"], 1)
                act.activation(pr[:, :, 1, :], pr[:, :, 1, :], ACT.Exp, scale=10.0).then_inc(S["probs_rdy"], 1)

            def silu(q, c):
                m = CHUNKS * q + c
                act.wait_ge(S["g_full"], m + 1)
                if m >= 2:
                    act.wait_ge(S["h_done"], m - 1)
                act.activation(s_buf[:, m % 2, :], pG[m % 2][:], ACT.Silu).then_inc(S["silu_done"], 1)

            def front_z(j):
                act.wait_ge(S["ln_T"], LN["front", j] + 1)
                if j == 0:
                    act.wait_ge(S["wo_full"], BLOCKS)
                    act.wait_ge(S["bias_rdy"], 1)
                else:
                    act.wait_ge(S["block_done"], j)
                    act.wait_ge(S["kept"], 64 * j)
                act.activation(zb[:], pA[:], ACT.Copy).then_inc(S["ln_out"], 1)
                step.inc(act.activation(hid[0:96, 3, :], ones[0:96, 0:1].broadcast_to((96, BT)), ACT.Copy))

            def front_hidden(j, k):
                act.wait_ge(S["hid_full"], 6 * j + k + 1)
                src = (pA, pB)[k % 2]
                if k == 3:
                    step.wait()
                    for r in range(3):
                        ins = act.activation(hid[32 * r:32 * r + ER, k, :], src[32 * r:32 * r + ER, :], ACT.Gelu,
                                             bias=b_b1[32 * r:32 * r + ER, k:k + 1])
                    ins.then_inc(S["hid_rdy"], 1)
                else:
                    m = LOW if k == 5 else P
                    act.activation(hid[0:m, k, :], src[0:m, :], ACT.Gelu if k < 3 else ACT.Identity,
                                   bias=b_b1[0:m, k:k + 1]).then_inc(S["hid_rdy"], 1)

            def front_tokens(j, i):
                t = G * j + i
                act.wait_ge(S["tokA_full"], t + 1)
                act.activation(rkv[:, i].rearrange("p r c -> p (r c)"), pA[:, 0:3 * C], ACT.Copy).then_inc(S["tokA_used"], 1)
                act.wait_ge(S["tokB_full"], t + 1)
                act.activation(low3[:, i].rearrange("p r c -> p (r c)"), pB[:, 0:3 * C], ACT.Copy).then_inc(S["tokB_used"], 1)

            def front_squash(j):
                act.wait_ge(S["tokB_used"], G * (j + 1))
                step.inc(act.activation(td, td, ACT.Tanh))
                step.inc(act.activation(rate, rate, ACT.Tanh, scale=0.5))
                step.inc(act.activation(gate, gate, ACT.Tanh, scale=0.5))
                step.wait()
                act.activation(td, td, ACT.Tanh, scale=0.5).then_inc(S["squashed"], 1)

            def front_decay(j):
                act.wait_ge(S["ew_log"], j + 1)
                act.activation(cumdec[:, 1:G + 1, :], logdec[:, 1:G + 1, :], ACT.Exp, scale=-DECAY / 2).then_inc(S["ew_exp"], 1)
                act.activation(invdec[:], logdec[:, 1:G + 1, :], ACT.Exp, scale=DECAY / 2).then_inc(S["ew_exp"], 1)

            def finish(u):
                for half, bank in enumerate((pA, pB)):
                    act.wait_ge(S["fin_full"], 4 * u + half + 1)
                    ins = act.activation(trans_T.rearrange("p (c i) -> p i c", i=N)[:, 4 * half:4 * half + 4, :],
                                         bank[:].rearrange("p (i c) -> p i c", i=4), ACT.Copy)
                    if half == 0:
                        step.inc(ins)
                ins.then_inc(S["trans_copied"], 1)
                for half, bank in enumerate((pA, pB)):
                    act.wait_ge(S["fin_full"], 4 * u + half + 3)
                    ins = act.activation(local_T.rearrange("p (c b k) -> p k b c", b=B, k=N)[:, 4 * half:4 * half + 4],
                                         bank[:].rearrange("p (k b c) -> p k b c", k=4, b=B), ACT.Copy)
                    if half == 0:
                        step.inc(ins)
                ins.then_inc(S["fin_copied"], 1)

            def link(u, c):
                n = NCH * u + c
                act.wait_ge(S["link_full"], n + 1)
                dst = states[:, c + 1] if c + 1 < NCH else last_state[:]
                act.activation(dst, (pA, pB)[n // PIECE % 2][:, n % PIECE * B * N:(n % PIECE + 1) * B * N].rearrange("p (b k) -> p b k", b=B),
                               ACT.Copy).then_inc(S["link_rdy"], 1)

            def starts(u):
                for half, bank in enumerate((pA, pB)):
                    act.wait_ge(S["w0_full"], 2 * u + half + 1)
                    act.activation(w0_sb[:, 512 * half:512 * half + 512], bank[:], ACT.Copy).then_inc(S["w0_rdy"], 1)

            def back_z(j):
                act.wait_ge(S["ln_T"], LN["back", j] + 1)
                act.activation(zb_out, pA[:], ACT.Copy).then_inc(S["ln_out"], 1)
                step.inc(act.activation(out_hid[0:32, 1, :], ones[0:32, 0:1].broadcast_to((32, BT)), ACT.Copy))

            def back_hidden(j):
                act.wait_ge(S["o_hid_full"], j + 1)
                step.wait()
                step.inc(act.activation(out_hid[:, 0, :], pA[:], ACT.Gelu, bias=col("ob1")))
                step.wait()
                act.activation(out_hid[0:ER, 1, :], pB[0:ER, :], ACT.Gelu, bias=b_b1r[0:ER, 1:2]).then_inc(S["o_hid_rdy"], 1)

            def run(task, *n):
                if task == "split":
                    split_high(*n)
                elif task == "in_z":
                    in_z(*n)
                elif task == "kvr":
                    copy_k(*n)
                elif task == "mid_z":
                    mid_z(*n)
                elif task == "ffn_z":
                    ffn_z(*n)
                elif task == "logits":
                    ffn_exp(*n)
                elif task == "front_z":
                    front_z(*n)
                elif task == "front_hidden":
                    front_hidden(*n)
                elif task == "front_tokens":
                    front_tokens(*n)
                elif task == "squash":
                    front_squash(*n)
                elif task == "decay":
                    front_decay(*n)
                elif task == "finish_T":
                    finish(*n)
                elif task == "link":
                    link(*n)
                elif task == "starts":
                    starts(*n)
                elif task == "back_z":
                    back_z(*n)
                elif task == "back_hidden":
                    back_hidden(*n)

            def weigh_expert(q, e, half):
                eg = E * q + e
                if half == 0:
                    act.wait_ge(S["y_full"], eg + 1)
                    if e == 0:
                        act.wait_ge(S["cw_rdy"], q + 1)
                    if eg >= 1:
                        act.wait_ge(S["x_added"], eg)
                for i in range(2 * half, 2 * half + 2):
                    ins = act.activation(y_weighted[:, i * P:(i + 1) * P], pY[eg % 2][:, i * P:(i + 1) * P], ACT.Identity,
                                         scale=cw[:, q % 2, i, e:e + 1])
                    if i < G - 1:
                        step.inc(ins)
                if half == 1:
                    ins.then_inc(S["y_scaled"], 1)

            setup()
            for t in PROLOGUE:
                run(*t)
            for g in range(len(SIDE)):
                early = 1 if len(LINKS[g]) > 2 else 0
                for n in LINKS[g][:early]:
                    link(*n)
                silu(*divmod(g, CHUNKS))
                for n in LINKS[g][early:2]:
                    link(*n)
                if g > FC and g % FC >= 2:
                    weigh_expert(*divmod(g // FC - 1, E), g % FC - 2)
                for n in LINKS[g][2:]:
                    link(*n)
                for t in SIDE[g]:
                    run(*t)

            for half in range(2):
                weigh_expert(2 * BLOCKS - 1, E - 1, half)

        @block.tensor
        def _(pe):
            def mm(dst, lhs, rhs, start=True, stop=True, **kw):
                return pe.matmul(dst, lhs, rhs, start=start, stop=stop, **kw)

            free = {}

            def take(bank):
                if bank in free:
                    pe.wait_ge(*free[bank])

            def ln_transposes(kind, j):
                n = LN[kind, j]
                name = bank_name(kind + "_z", j)
                pe.wait_ge(S["ln_norm"], n + 1)
                take(name)
                for i in range(G):
                    ins = pe.transpose(bank_named[name][:, i * P:(i + 1) * P], normed[:, n % 2, i, :], ident[:])
                ins.then_inc(S["ln_T"], 1)
                free[name] = (S["ln_out"], n + 1)

            def kvr(s):
                if s == 0:
                    pe.wait_ge(S["w_in_a"], 16 * 5)
                pe.wait_ge(S["mixed_rdy"], s + 1)
                for i, part in enumerate("kvr"):
                    name = bank_name(part, s)
                    take(name)
                    ins = mm(bank_named[name][:], w_a[:, i, :], mixed[:, i, :])
                    free[name] = (S[("k_copied", "kv_read", "kvr_used")[i]], s + 1)
                    if i == 1:
                        ins.then_inc(S["kv_full"], 1)
                ins.then_inc(S["kvr_full"], 1)

            def mid_tokens(q):
                u, g = divmod(q, BU)
                name = bank_name("mid_T", q)
                pe.wait_ge(S["kvr_used"], B * (u + 1))
                take(name)
                for i in range(G):
                    ins = pe.transpose(bank_named[name][:, i * P:(i + 1) * P],
                                       oT.rearrange("c (u p i) -> c u i p", u=UNITS, i=LU)[:, u, G * g + i, :], ident[:])
                ins.then_inc(S["ot_full"], 1)
                free[name] = (S["inner_read"], q + 1)

            def mid_out(q):
                name = bank_name("mid_out", q)
                pe.wait_ge(S["ln_out"], LN["mid", q] + 1)
                take(name)
                for i in range(G):
                    ins = mm(bank_named[name][:, i * P:(i + 1) * P], nT[:, i * P:(i + 1) * P], w_a[:, 3, :])
                ins.then_inc(S["wo_full"], 1)
                free[name] = (S["x1_rdy"], q + 1)

            def biases():
                pe.wait_ge(S["w_in_b"], 16 * (18 + 1 + 8 + 4 + len(ROWS)))
                take("B")
                for k, mu in enumerate(("mu_r", "mu_k", "mu_v")):
                    mm(pB[:, k:k + 1], b_w1[:, k, :], col(mu))
                for i, mu in enumerate(("mu_r", "mu_k", "mu_v")):
                    mm(pB[32 * i:32 * i + 32, 3:4], b_w1[:, 3, 32 * i:32 * i + 32], col(mu))
                mm(pB[0:LOW, 4:5], b_w1[:, 4, 0:LOW], col("mu_d"))
                mm(pB[LOW:P, 4:5], b_w1[:, 4, LOW:P], col("mu_a"))
                mm(pB[0:LOW, 5:6], b_w1[:, 5, 0:LOW], col("mu_g")).then_inc(S["bias_full"], 1)
                free["B"] = (S["bias_rdy"], 1)

            def router(q):
                if q == 0:
                    pe.wait_ge(S["w_in_f"], 16 * 3)
                pe.wait_ge(S["ln_out"], LN["ffn", q] + 1)
                take("B")
                for i in range(G):
                    ins = mm(pB[:, 2 * E * i:2 * E * i + 2 * E], zf[:, i * P:(i + 1) * P], w_router[:])
                ins.then_inc(S["rl_full"], 1)
                free["B"] = (S["rl_used"], q + 1)

            def down(m, half):
                e, f = divmod(m, FC)
                pe.wait_ge(S["h_done"], m + 1)
                if f == 0 and half == 0:
                    if e >= 2:
                        pe.wait_ge(S["y_scaled"], e - 1)
                    else:
                        take(f"Y{e}")
                for i in range(2 * half, 2 * half + 2):
                    ins = mm(pY[e % 2][:, i * P:(i + 1) * P], h_buf[:, m % 4, i * P:(i + 1) * P], w_down[:, e % E, f, :],
                             start=(f == 0 and i == 0), stop=(f == FC - 1), skip_group_check=True)
                if half == 1:
                    ins.then_inc(S["y_full" if f == FC - 1 else "d_done"], 1)

            def split_product(bank, lo, hi, z):
                mm(bank, hi, z_lo[:, z, :], stop=False)
                mm(bank, lo, z_hi[:, z, :], start=False, stop=False)
                return mm(bank, hi, z_hi[:, z, :], start=False)

            def local_part(piece):
                name = "AB"[piece % 2]
                take(name)
                first = (piece % PIECES) * PIECE * B * N
                mm(bank_named[name][:, 0:PIECE * B * N], ident[:], local_T[:, first:first + PIECE * B * N],
                   stop=False, skip_group_check=True)

            def link(u, c):
                n = NCH * u + c
                piece, k = divmod(n, PIECE)
                if c == 0:
                    pe.wait_ge(S["fin_copied"], u + 1)
                    pe.wait_ge(S["first_rdy"], u + 1)
                    local_part(piece)
                else:
                    pe.wait_ge(S["link_rdy"], n)
                if k == 0:
                    pe.wait_ge(S["bd_rdy"], piece + 1)
                bd = tr.rearrange("p (w b c m) -> p w b c m", w=2, b=B, c=PIECE)
                bank = (pA, pB)[piece % 2]
                for b in range(B):
                    ins = mm(bank[:, (k * B + b) * N:(k * B + b + 1) * N], bd[:, piece % 2, b, k, :], states[:, c, b, :],
                             start=False, skip_group_check=True)
                ins.then_inc(S["link_full"], 1)
                if k == PIECE - 1:
                    free["AB"[piece % 2]] = (S["link_rdy"], n + 1)
                    if c + 1 < NCH:
                        local_part(piece + 1)

            def finish(u):
                pe.wait_ge(S["fin_rdy"], 2 * (u + 1))
                lf = locst[:].rearrange("p (hi k) -> p k hi", k=N)
                for part, copied in enumerate(("trans_copied", "fin_copied")):
                    for i in range(N):
                        if i % 4 == 0:
                            take("AB"[i // 4])
                        src = outer[:, i * P:(i + 1) * P] if part == 0 else lf[:, i]
                        ins = pe.transpose((pA, pB)[i // 4][:, (i % 4) * P:(i % 4 + 1) * P], src, ident[:])
                        if i % 4 == 3:
                            ins.then_inc(S["fin_full"], 1)
                    free["A"] = free["B"] = (S[copied], u + 1)

            def starts(u):
                pe.wait_ge(S["link_rdy"], NCH * (u + 1))
                take("A")
                take("B")
                for k in range(N):
                    for b in range(B):
                        ins = mm((pA, pB)[k // 4][b * NCH:(b + 1) * NCH, (k % 4) * P:(k % 4 + 1) * P],
                                 states[:, :, b, k], ident[:])
                    if k % 4 == 3:
                        ins.then_inc(S["w0_full"], 1)
                free["A"] = free["B"] = (S["w0_rdy"], 2 * (u + 1))

            def split_product(bank, lo, hi, z):
                mm(bank, hi, z_lo[:, z, :], stop=False)
                mm(bank, lo, z_hi[:, z, :], start=False, stop=False)
                return mm(bank, hi, z_hi[:, z, :], start=False)

            def chunk(g):
                q, c = divmod(g, CHUNKS)
                e, f = divmod(c, FC)
                cols_f = slice(f * P, (f + 1) * P)
                chain = list(LINKS[g])
                if c == 0:
                    pe.wait_ge(S["z_low"], q + 1)
                if g == 0:
                    for i in (2 * E - 2, 2 * E - 1):
                        pe.wait_ge(w_split[splitter(i)[0]], splitter(i)[1])
                if g >= 2:
                    pe.wait_ge(S["silu_done"], g - 1)
                else:
                    take(f"G{g}")
                split_product(pG[g % 2][:], w_lo[:, e, 0, cols_f], w_hi[:, e, 0, cols_f], q % 2).then_inc(S["g_full"], 1)
                if len(chain) > 2:
                    link(*chain.pop(0))
                if g >= 2:
                    pe.wait_ge(S["h_done"], g - 1)
                else:
                    take(f"U{g}")
                split_product(pU[g % 2][:], w_lo[:, e, 1, cols_f], w_hi[:, e, 1, cols_f], q % 2).then_inc(S["u_full"], 1)
                if len(chain) > 1:
                    link(*chain.pop(0))
                if g >= LAG:
                    down(g - LAG, 0)
                    if len(chain) > 1:
                        link(*chain.pop(0))
                    down(g - LAG, 1)
                for n in chain:
                    link(*n)

            def front_hidden(j, k):
                take("AB"[k % 2])
                m = (P, P, P, 96, P, LOW)[k]
                mm((pA, pB)[k % 2][0:m, :], b_w1[:, k, 0:m], zb[:]).then_inc(S["hid_full"], 1)
                free["AB"[k % 2]] = (S["hid_rdy"], 6 * j + k + 1)

            def front_tokens(j, i):
                t = G * j + i
                tok = slice(i * P, (i + 1) * P)
                pe.wait_ge(S["hid_rdy"], 6 * j + 6)
                take("A")
                mm(pA[:, 0:3 * C], hid[0:96, 3, tok], b_w2r[0:96].rearrange("p r c -> p (r c)"), stop=False)
                for r in range(3):
                    ins = mm(pA[:, r * C:(r + 1) * C], hid[:, r, tok], b_w2[:, r, :], start=False, stop=(r == 2))
                ins.then_inc(S["tokA_full"], 1)
                free["A"] = (S["tokA_used"], t + 1)
                take("B")
                mm(pB[:, 0:2 * C], hid[:, 4, tok], b_low[:, 0:2, :].rearrange("p r c -> p (r c)"), stop=False)
                mm(pB[:, 0:2 * C], ones[0:1, :], b_row[0:1, :], start=False)
                mm(pB[:, 2 * C:3 * C], hid[0:LOW, 5, tok], b_low[0:LOW, 2, :]).then_inc(S["tokB_full"], 1)
                free["B"] = (S["tokB_used"], t + 1)

            def back_hidden(j):
                pe.wait_ge(S["ln_out"], LN["back", j] + 1)
                take("A")
                take("B")
                mm(pA[:], b_ow1[:, 0:P], zb_out)
                mm(pB[0:ER, :], b_ow1[:, P:EH], zb_out).then_inc(S["o_hid_full"], 1)
                free["A"] = free["B"] = (S["o_hid_rdy"], j + 1)

            def back_out(j):
                take("A")
                for i in range(G):
                    tok = slice(i * P, (i + 1) * P)
                    mm(pA[:, tok], out_hid[:, 0, tok], b_w2[:, 3, :], stop=False)
                    ins = mm(pA[:, tok], out_hid[0:ER + 1, 1, tok], b_o2r[0:ER + 1, :], start=False)
                ins.then_inc(S["o_full"], 1)
                free["A"] = (S["x3_rdy"], j + 1)

            def run(task, *n):
                if task in ("in_z", "mid_z", "ffn_z", "front_z", "back_z"):
                    ln_transposes(task[:-2], *n)
                elif task == "kvr":
                    kvr(*n)
                elif task == "mid_T":
                    mid_tokens(*n)
                elif task == "mid_out":
                    mid_out(*n)
                elif task == "biases":
                    biases()
                elif task == "route":
                    router(*n)
                elif task == "front_hidden":
                    front_hidden(*n)
                elif task == "front_tokens":
                    front_tokens(*n)
                elif task == "finish_T":
                    finish(*n)
                elif task == "link":
                    link(*n)
                elif task == "starts":
                    starts(*n)
                elif task == "back_hidden":
                    back_hidden(*n)
                elif task == "back_out":
                    back_out(*n)

            pe.wait_ge(S["const"], 1)
            for t in PROLOGUE:
                run(*t)
            for g in range(len(SIDE)):
                chunk(g)
                for t in SIDE[g]:
                    run(*t)
            for g in range(len(SIDE) - LAG, len(SIDE)):
                down(g, 0)
                down(g, 1)

        @block.vector
        def _(dve):
            step = Count(dve, S["dve_step"])

            def ln_stats(n, tiles):
                if n >= 2:
                    dve.wait_ge(S["ln_T"], n - 1)
                for i in range(G):
                    step.inc(dve.bn_stats(stats[:, n % 2, i, :], tiles[:, i, :]))
                step.wait()
                for i in range(G):
                    ins = dve.bn_aggr(mean_var[:, n % 2, i, :], stats[:, n % 2, i, :])
                    if i < G - 1:
                        step.inc(ins)
                ins.then_inc(S["ln_mv"], 1)

            def ln_normalise(n, tiles, last_sem="ln_norm"):
                dve.wait_ge(S["ln_rstd"], n + 1)
                for i in range(G):
                    ins = dve.tensor_scalar(normed[:, n % 2, i, :], tiles[:, i, :], mean_var[:, n % 2, i, 0:1],
                                            rstd[:, n % 2, i:i + 1], ALU.subtract, ALU.mult)
                    if i < G - 1 or not last_sem:
                        step.inc(ins)
                if last_sem:
                    ins.then_inc(S[last_sem], 1)

            def xt(j):
                return x[:, G * j:G * j + G, :]

            def mix(s):
                u, b = divmod(s, B)
                if b == 0:
                    dve.wait_ge(S["ln_out"], LN["in", BU * u + BU - 1] + 1)
                if s == 0:
                    dve.wait_ge(S["w_in_a"], 16 * 5)
                cur, prev = xn[:, b, 1 + u * TU:1 + (u + 1) * TU], xn[:, b, u * TU:(u + 1) * TU]
                step.inc(dve.tensor_tensor(diff[:, s % 2, :], cur, prev, ALU.subtract))
                step.wait()
                if s >= 1:
                    dve.wait_ge(S["kvr_full"], s)
                for i, nm in enumerate(("mix_k", "mix_v", "mix_r")):
                    ins = dve.scalar_tensor_tensor(out=mixed[:, i, :], in0=diff[:, s % 2, :], scalar=col(nm), in1=prev,
                                                   op0=ALU.mult, op1=ALU.add)
                    if i < 2:
                        step.inc(ins)
                ins.then_inc(S["mixed_rdy"], 1)

            def scan(s):
                u, b = divmod(s, B)
                if s == 0:
                    dve.wait_ge(S["decay_rdy"], 1)
                dve.wait_ge(S["k_copied"], s + 1)
                dve.tensor_tensor(kv[:, s % 2, :], k_sb, bank_of("v", s)[:], ALU.mult).then_inc(S["kv_read"], 1)
                dve.wait_ge(S["kv_read"], s + 1)
                step.inc(dve.tensor_tensor_scan(st_a[:, s % 2, :], decay_a[:].broadcast_to((P, BT)), kv[:, s % 2, :],
                                                0.0 if u == 0 else scan_end[:, b:b + 1], ALU.mult, ALU.add))
                step.wait()
                step.inc(dve.tensor_copy(scan_end[:, b:b + 1], st_a[:, s % 2, BT - 1:BT]))
                step.inc(dve.scalar_tensor_tensor(out=diff[:, s % 2, :], in0=kv[:, s % 2, :], scalar=col("first"),
                                                  in1=st_a[:, s % 2, :], op0=ALU.mult, op1=ALU.add))
                step.wait()
                dve.wait_ge(S["kvr_full"], s + 1)
                dve.tensor_tensor(oT[:, s * BT:(s + 1) * BT], diff[:, s % 2, :], bank_of("r", s)[:],
                                  ALU.mult).then_inc(S["kvr_used"], 1)
                dve.wait_ge(S["kvr_used"], s + 1)

            def inner(q):
                return bank_of("mid_T", q)[:].rearrange("p (i c) -> p i c", i=G)

            def mid_norm(q):
                ln_normalise(LN["mid", q], inner(q), None)
                step.wait()
                dve.tensor_scalar(tmp[:, 0, 0:1], neg_half[:], 1.0, None, ALU.mult).then_inc(S["inner_read"], 1)
                dve.tensor_scalar(tmp[:, 0, 1:2], neg_half[:], 1.0, None, ALU.mult).then_inc(S["ln_norm"], 1)

            def mid_add(q):
                dve.wait_ge(S["wo_full"], q + 1)
                dve.tensor_tensor(xt(q), xt(q), bank_of("mid_out", q)[:].rearrange("p (i c) -> p i c", i=G),
                                  ALU.add).then_inc(S["x1_rdy"], 1)
                dve.wait_ge(S["x1_rdy"], q + 1)

            def softmax_logits(q):
                lg = pB[:, 0:G * 2 * E].rearrange("p (g e) -> p g e", e=E)
                dve.wait_ge(S["rl_full"], q + 1)
                step.inc(dve.tensor_reduce(lmax[:], lg, AX_X, ALU.max))
                step.wait()
                dve.tensor_tensor(probs[:], lg, lmax[:].unsqueeze(2).broadcast_to((P, 2 * G, E)),
                                  ALU.subtract).then_inc(S["rl_used"], 1)

            def combine_weights(q):
                w = cw[:, q % 2]
                dve.wait_ge(S["probs_rdy"], 2 * q + 2)
                if q >= 2:
                    dve.wait_ge(S["y_scaled"], E * (q - 1))
                pr = probs[:].rearrange("p (g s) e -> p g s e", s=2)
                step.inc(dve.tensor_reduce(psum_[:], probs[:], AX_X, ALU.add))
                step.inc(dve.tensor_tensor(w, pr[:, :, 0, :], pr[:, :, 1, :], ALU.mult))
                step.wait()
                step.inc(dve.reciprocal(prec[:], psum_[:]))
                step.wait()
                pc = prec[:].rearrange("p (g s) -> p g s", s=2)
                step.inc(dve.tensor_tensor(pscale[:], pc[:, :, 0], pc[:, :, 1], ALU.mult))
                step.wait()
                step.inc(dve.tensor_tensor(w, w, pscale[:].unsqueeze(2).broadcast_to((P, G, E)), ALU.mult))
                step.wait()
                step.inc(dve.tensor_reduce(cwsum[:], w, AX_X, ALU.add))
                step.wait()
                step.inc(dve.tensor_scalar(cwsum[:], cwsum[:], 1e-9, None, ALU.add))
                step.wait()
                step.inc(dve.reciprocal(pscale[:], cwsum[:]))
                step.wait()
                dve.tensor_tensor(w, w, pscale[:].unsqueeze(2).broadcast_to((P, G, E)), ALU.mult).then_inc(S["cw_rdy"], 1)

            def hidden(q, c):
                m = CHUNKS * q + c
                dve.wait_ge(S["silu_done"], m + 1)
                dve.wait_ge(S["u_full"], m + 1)
                if m >= 4:
                    done = m - 3
                    if done % FC == 0:
                        dve.wait_ge(S["y_full"], done // FC)
                    else:
                        dve.wait_ge(S["d_done"], (FC - 1) * (done // FC) + done % FC)
                dve.tensor_tensor(h_buf[:, m % 4, :], s_buf[:, m % 2, :], pU[m % 2][:], ALU.mult).then_inc(S["h_done"], 1)

            def by_head(v):
                return v.rearrange("p g (h n) -> p g h n", n=N)

            def spread(v):
                return v.rearrange("p (g h) -> p g h", g=G).unsqueeze(3).broadcast_to((P, G, H, N))

            def front_log(j):
                dve.wait_ge(S["squashed"], j + 1)
                if j >= 1:
                    dve.wait_ge(S["kept"], 64 * j)
                step.inc(dve.tensor_copy(logdec[:, 0, :], logdec[:, G, :]))
                step.inc(dve.tensor_copy(cumdec[:, 0, :], cumdec[:, G, :]))
                for i in range(G):
                    step.wait()
                    ins = dve.scalar_tensor_tensor(out=logdec[:, i + 1, :], in0=td[:, i, :], scalar=1.0,
                                                   in1=logdec[:, i, :], op0=ALU.add, op1=ALU.add)
                    if i < G - 1:
                        step.inc(ins)
                ins.then_inc(S["ew_log"], 1)

            def front_keys(j):
                step.inc(dve.tensor_tensor(rem[:], kk, row("rem"), ALU.mult))
                step.wait()
                step.inc(dve.tensor_tensor(scr[:], rem[:], rem[:], ALU.mult))
                step.inc(dve.scalar_tensor_tensor(out=bh[:], in0=rate, scalar=1.0, in1=rem[:], op0=ALU.add, op1=ALU.mult))
                step.wait()
                step.inc(dve.tensor_reduce(ss[:], by_head(scr[:]), AX_X, ALU.add))
                step.inc(dve.scalar_tensor_tensor(out=rate, in0=rate, scalar=-1.0, in1=row("mix"), op0=ALU.add, op1=ALU.mult))
                step.wait()
                step.inc(dve.tensor_scalar(ss[:], ss[:], 1e-24, None, ALU.max))
                step.inc(dve.scalar_tensor_tensor(out=kk, in0=rate, scalar=1.0, in1=kk, op0=ALU.add, op1=ALU.mult))
                step.wait()
                step.inc(dve.reciprocal(ss[:], ss[:]))

            def front_bonus(j):
                step.inc(dve.tensor_tensor(scr[:], recept, kk, ALU.mult))
                step.wait()
                step.inc(dve.tensor_reduce(bs[:], by_head(scr[:]), AX_X, ALU.add))
                step.inc(dve.tensor_tensor(local[:], vv, row("bonus"), ALU.mult))
                step.wait()
                step.inc(dve.tensor_tensor(by_head(local[:]), by_head(local[:]), spread(bs[:]), ALU.mult))

            def front_scale(j):
                dve.wait_ge(S["ew_exp"], 2 * j + 2)
                step.inc(dve.scalar_tensor_tensor(out=bh[:], in0=bh[:], scalar=0.5, in1=cumdec[:, 0:G, :], op0=ALU.mult, op1=ALU.mult))
                step.inc(dve.tensor_tensor(kh[:], rem[:], invdec[:], ALU.mult))
                step.inc(dve.tensor_tensor(vv, vv, invdec[:], ALU.mult))
                step.wait()
                dve.tensor_tensor(by_head(kh[:]), by_head(kh[:]), spread(ss[:]), ALU.mult).then_inc(S["front_rdy"], 1)
                dve.wait_ge(S["front_rdy"], j + 1)

            p3 = prod.rearrange("p (hi c) -> p hi c", c=2 * N)
            loc3 = locst[:].rearrange("p (hi k) -> p hi k", k=N)

            def read_sum(j, i):
                dve.wait_ge(S["readout_rdy"], G * j + i + 1)
                dve.tensor_reduce(scr[:, i, :], readout[:].rearrange("p (hi k) -> p hi k", k=N), AX_X, ALU.add)\
                   .then_inc(S["readout_used"], 1)

            def step_part(j, i, part):
                t = G * j + i
                if t % LU == 0 and part < 3:
                    if part == 1:
                        step.inc(dve.memset(tmp[:, :, 0:N], 0.0))
                        dve.tensor_copy(tmp[:, :, N:2 * N], bh[:, i, :].rearrange("p (h j) -> p h j", h=H)).then_inc(S["tmp_rdy"], 1)
                elif part == 0:
                    if t >= 1:
                        dve.wait_ge(S["step_upd"], t)
                        dve.wait_ge(S["trans_rdy"], t)
                    bb = bh[:, i, :].unsqueeze(2).broadcast_to((P, H * N, N))
                    step.inc(dve.tensor_tensor(p3[:, :, 0:N], loc3, bb, ALU.mult))
                    step.inc(dve.tensor_tensor(p3[:, :, N:2 * N], trans[:, (i - 1) % G, :].rearrange("p (hi k) -> p hi k", k=N),
                                               bb, ALU.mult))
                elif part == 1:
                    step.wait()
                    dve.tensor_reduce(tmp[:], prod.rearrange("p (h i c) -> p h c i", h=H, i=N), AX_X, ALU.add)\
                       .then_inc(S["tmp_rdy"], 1)
                elif part == 2:
                    dve.wait_ge(S["tmp_rdy"], t + 1)
                    step.inc(dve.tensor_tensor(prod.rearrange("p (h i c) -> p h i c", h=H, i=N)[:, :, :, 0:N],
                                               kh[:, i, :].rearrange("p (h i) -> p h i", h=H).unsqueeze(3).broadcast_to((P, H, N, N)),
                                               tmp[:, :, 0:N].unsqueeze(2).broadcast_to((P, H, N, N)), ALU.mult))
                    step.wait()
                    if t >= 1:
                        dve.wait_ge(S["readout_rdy"], t)
                    step.inc(dve.tensor_tensor(loc3, loc3, p3[:, :, 0:N], ALU.subtract))
                else:
                    dve.wait_ge(S["outer_rdy"], t + 1)
                    step.wait()
                    dve.tensor_tensor(locst[:], locst[:], outer, ALU.add).then_inc(S["step_upd"], 1)
                    if i >= 1:
                        read_sum(j, i - 1)

            def block_end(j):
                read_sum(j, G - 1)
                dve.wait_ge(S["readout_used"], G * (j + 1))
                step.inc(dve.tensor_tensor(scr[:], scr[:], cumdec[:, 1:G + 1, :], ALU.mult))
                step.wait()
                dve.tensor_tensor(local[:], local[:], scr[:], ALU.add).then_inc(S["block_done"], 1)
                dve.wait_ge(S["block_done"], j + 1)
                dve.wait_ge(S["step_upd"], G * (j + 1))
                dve.wait_ge(S["trans_rdy"], G * (j + 1))

            def biases():
                dve.wait_ge(S["bias_full"], 1)
                for k, nm in enumerate(("rb1", "kb1", "vb1")):
                    step.inc(dve.tensor_tensor(b_b1[:, k:k + 1], pB[:, k:k + 1], col(nm), ALU.add))
                step.inc(dve.tensor_tensor(b_b1[0:96, 3:4], pB[0:96, 3:4], b_b1r[0:96, 0:1], ALU.add))
                step.inc(dve.tensor_copy(b_b1[:, 4:5], pB[:, 4:5]))
                step.inc(dve.tensor_scalar(rows[:, 2, :], rows[:, 2, :], 0.2, None, ALU.mult))
                step.inc(dve.tensor_scalar(rows[:, 1, :], rows[:, 1, :], 0.5, None, ALU.mult))
                step.inc(dve.tensor_scalar(rows[:, 3:5, :], rows[:, 3:5, :], 0.5, None, ALU.mult))
                restart()
                step.wait()
                dve.tensor_copy(b_b1[0:LOW, 5:6], pB[0:LOW, 5:6]).then_inc(S["bias_rdy"], 1)

            def restart():
                step.inc(dve.memset(locst[:], 0.0))
                step.inc(dve.memset(cumdec[:, G, :], 1.0))
                step.inc(dve.memset(logdec[:, G, :], 0.0))
                last = trans[:, G - 1, :].rearrange("p (h ij) -> p h ij", h=H)
                step.inc(dve.memset(last, 0.0))
                step.wait()
                step.inc(dve.memset(last[:, :, 0:N * N:N + 1], 1.0))
                step.wait()

            def finish(u):
                dve.wait_ge(S["trans_rdy"], LU * (u + 1))
                dend = cumdec[:, G, :].unsqueeze(2).broadcast_to((P, C, N))
                tfin = trans[:, G - 1, :].rearrange("p (c k) -> p c k", k=N)
                dve.tensor_tensor(outer.rearrange("p (i h j) -> p h i j", i=N, h=H), tfin.rearrange("p (h i) j -> p h i j", h=H),
                                  dend.rearrange("p (h i) j -> p h i j", h=H), ALU.mult).then_inc(S["fin_rdy"], 1)
                lv = locst[:].rearrange("p (c k) -> p c k", k=N)
                dve.tensor_tensor(lv, lv, dend, ALU.mult).then_inc(S["fin_rdy"], 1)
                if u == 0:
                    dve.memset(states[:, 0], 0.0).then_inc(S["first_rdy"], 1)
                else:
                    dve.wait_ge(S["link_rdy"], NCH * u)
                    dve.tensor_copy(states[:, 0], last_state[:]).then_inc(S["first_rdy"], 1)

            w0 = w0_sb.rearrange("p (k h j) -> p h j k", k=N, h=H)
            ta = readout[:]
            ta4 = ta.rearrange("p (h j k) -> p h j k", h=H, j=N)

            def back_part(j, i, part):
                if i == 0 and part == 0:
                    if j >= 1:
                        dve.wait_ge(S["o_full"], j)
                    dve.wait_ge(S["w0_rdy"], 2 * (j // BU + 1))
                    dve.wait_ge(S["keep_in"], 16 * (j + 1))
                if part == 0:
                    step.inc(dve.tensor_tensor(ta4, w0, over_i(keep[:, 0, i, :]), ALU.mult))
                    step.wait()
                    dve.tensor_reduce(bh[:, i, :], ta.rearrange("p (hj k) -> p hj k", k=N), AX_X, ALU.add).then_inc(S["y0_rdy"], 1)
                    dve.wait_ge(S["y0_rdy"], G * j + i + 1)
                else:
                    dve.wait_ge(S["y1_rdy"], G * j + i + 1)
                    dve.tensor_reduce(scr[:, i, :], trans[:, i, :].rearrange("p (hi j) -> p hi j", j=N), AX_X, ALU.add).then_inc(S["y1_used"], 1)

            def back_sum(j):
                dve.wait_ge(S["y1_used"], G * (j + 1))
                step.inc(dve.tensor_tensor(scr[:], scr[:], keep[:, 3], ALU.mult))
                step.wait()
                step.inc(dve.tensor_tensor(scr[:], scr[:], keep[:, 2], ALU.add))
                step.wait()
                ln_stats(LN["back", j], scr[:])

            def back_norm(j):
                n = LN["back", j]
                ln_normalise(n, scr[:], None)
                step.wait()
                nm = normed[:, n % 2]
                step.inc(dve.tensor_tensor(nm, nm, row("ln_g"), ALU.mult))
                step.wait()
                step.inc(dve.tensor_tensor(nm, nm, row("ln_b"), ALU.add))
                step.wait()
                dve.scalar_tensor_tensor(out=nm, in0=keep[:, 1], scalar=1.0, in1=nm, op0=ALU.add, op1=ALU.mult).then_inc(S["ln_norm"], 1)
                dve.wait_ge(S["ln_norm"], n + 1)
                dve.tensor_scalar(tmp[:, 0, 0:1], neg_half[:], 1.0, None, ALU.mult).then_inc(S["back_read"], 1)

            def back_add(j):
                dve.wait_ge(S["o_full"], j + 1)
                dve.tensor_tensor(xt(j), xt(j), pA[:].rearrange("p (i c) -> p i c", i=G), ALU.add).then_inc(S["x3_rdy"], 1)
                dve.wait_ge(S["x3_rdy"], j + 1)

            def run(task, *n):
                kind = task.split("_")[0]
                if task == "split":
                    i = n[0]
                    if splitter(i)[0] == 1:
                        dve.wait_ge(S["w_high"], i + 1)
                        dve.tensor_tensor(w_lo[:, i // 2, i % 2, :], sh_buf[:, i % 6, :], w_hi[:, i // 2, i % 2, :].bitcast(F32),
                                          ALU.subtract).then_inc(w_split[1], 1)
                elif task == "mid_stats":
                    dve.wait_ge(S["ot_full"], n[0] + 1)
                    ln_stats(LN["mid", n[0]], inner(n[0]))
                elif task == "mid_norm":
                    mid_norm(*n)
                elif task == "back_stats":
                    back_sum(*n)
                elif task == "back_norm":
                    back_norm(*n)
                elif task.endswith("_stats"):
                    if kind == "in" and n[0] % BU == 0:
                        dve.wait_ge(x_in[n[0] // BU], 16 * B)
                    if kind == "front":
                        dve.wait_ge(S["x_added"], E * (n[0] + 1))
                    ln_stats(LN[kind, n[0]], xt(n[0] % BLOCKS))
                elif task.endswith("_norm"):
                    ln_normalise(LN[kind, n[0]], xt(n[0] % BLOCKS))
                elif task == "mix":
                    mix(*n)
                elif task == "scan":
                    scan(*n)
                elif task == "mid_add":
                    mid_add(*n)
                elif task == "biases":
                    biases()
                elif task == "restart":
                    restart()
                elif task == "logits":
                    softmax_logits(*n)
                elif task == "combine":
                    combine_weights(*n)
                elif task == "log":
                    front_log(*n)
                elif task == "keys":
                    front_keys(*n)
                elif task == "bonus":
                    front_bonus(*n)
                elif task == "scale":
                    front_scale(*n)
                elif task == "step":
                    step_part(*n)
                elif task == "block_end":
                    block_end(*n)
                elif task == "finish":
                    finish(*n)
                elif task == "back_part":
                    back_part(*n)
                elif task == "back_add":
                    back_add(*n)

            for t in PROLOGUE:
                run(*t)
            for g in range(len(SIDE)):
                q, c = divmod(g, CHUNKS)
                hidden(q, c)
                for t in SIDE[g]:
                    run(*t)


A, BB, FF = "L0_attn_a_", "L0_attn_b_", "L0_ffn_"


def kernel(**inputs):
    import numpy as np
    import concourse.bacc as bacc
    from concourse.bass_utils import run_bass_kernel_spmd

    g = {k: np.asarray(v) for k, v in inputs.items()}
    col = [g[A + "time_mix_k"].reshape(C), g[A + "time_mix_v"].reshape(C), g[A + "time_mix_r"].reshape(C),
           g[A + "time_decay"].reshape(C), g[A + "time_first"].reshape(C), g[A + "ln_g"], g[A + "ln_b"]]
    col += [g[BB + "mu_" + n] for n in "rkvgad"]
    col += [g[BB + n + "b1"][0:P] for n in "rkvo"]
    arrays = {
        "x": g[A + "x"],
        "cols": np.ascontiguousarray(np.stack(col, axis=1)),
        "rows": np.stack([g[BB + n] for n in ("rem_mult", "iclr_mix", "bonus_mult", "ln_g", "ln_b")]),
    }
    for n in ("Wk", "Wv", "Wr", "Wo"):
        arrays[n] = np.ascontiguousarray(g[A + n].T)
    for n in ("dA", "dB", "db", "aA", "aB", "ab", "gA", "gB"):
        arrays[n] = g[BB + n]
    for n in "rkvo":
        for m in ("W1", "b1", "W2", "b2"):
            arrays[n + m] = g[BB + n + m]
    for n in ("w_router", "w_gating", "w_gate", "w_up", "w_down"):
        arrays[n] = g[FF + n]

    nc = bacc.Bacc("TRN2", target_bir_lowering=False, num_devices=1)
    aps = {n: nc.dram_tensor("in_" + n, v.shape, F32, kind="ExternalInput").ap() for n, v in arrays.items()}
    out = nc.dram_tensor("out", (B, T, C), F32, kind="ExternalOutput").ap()
    build(nc, aps, out)
    r = run_bass_kernel_spmd(nc, [{"in_" + n: v for n, v in arrays.items()}], core_ids=[0])
    return r.results[0]["out"]
```
